# Optimizing a Trainium2 kernel written in Bass

```python
import numpy as np
import jax
import jax.numpy as jnp

def _softmax(x, axis=-1):
    return jax.nn.softmax(x, axis=axis)

def _gelu(x):
    return jax.nn.gelu(x, approximate=True)

def _silu(x):
    return jax.nn.silu(x)

def _sigmoid(x):
    return jax.nn.sigmoid(x)

def _layernorm(x, axis=-1, eps=1e-05):
    m = jnp.mean(x, axis=axis, keepdims=True)
    v = jnp.var(x, axis=axis, keepdims=True)
    return (x - m) / jnp.sqrt(v + eps)

def _scatter_add(tgt, idx, src, axis=0):
    return tgt.at[idx].add(src)

def _segment_sum(src, seg, n):
    return jax.ops.segment_sum(src, seg, n)
kernel_name = 'mk_adj_preln_d4_adj_r2_be734c'

def setup_inputs(seed: int=0):
    np.random.seed(seed)
    _w = jnp.asarray

    def _rec_inputs():
        import jax
        import jax.numpy as jnp
        _gk = jax.random.key(seed)
        x = -0.0005207 + 1.001 * jax.random.normal(jax.random.fold_in(_gk, 1), (64, 128, 128), jnp.float32)
        _w = (1.0 + jnp.arange(128, dtype=jnp.float32)) ** (-0.5)
        _w = _w / _w.mean()
        _pij = jnp.clip(0.015625 * _w[:, None] * _w[None, :], 0.0, 1.0)
        _a = jax.random.uniform(jax.random.fold_in(_gk, 2), (64, 128, 128)) < _pij
        _af = _a.astype(jnp.float32)
        adj = _af
        _nm = jnp.ones((64, 128), dtype=bool)
        nodemask = jnp.where(_nm, 1.0, 0.0).astype(jnp.float32)
        return (x, adj, nodemask)
    x, adj, nodemask = _rec_inputs()

    def _L0_gnn_setup():
        import jax, jax.numpy as jnp
        import numpy as np
        B, N, IN_DIM, OUT_DIM, H = (8, 512, 128, 128, 4)
        D = OUT_DIM // H
        NEG_INF = -9000000000000000.0
        LRELU_SLOPE = 0.2
        key = jax.random.key(seed)
        k1, k2, k3, k4 = jax.random.split(key, 4)
        x = jax.random.normal(k1, (B, N, IN_DIM), dtype=jnp.float32)
        adj = jax.random.randint(k2, (B, N, N), 0, 2).astype(jnp.float32)
        W = jax.random.normal(k3, (IN_DIM, H * D), dtype=jnp.float32) * jnp.sqrt(2.0 / (IN_DIM + H * D))
        a = jax.random.normal(k4, (H, 2 * D), dtype=jnp.float32) * jnp.sqrt(2.0 / (H + 2 * D))
        return {'x': x, 'adj': adj, 'W': W, 'a': a}
    _L0_gnn_all = _L0_gnn_setup()
    _L0_gnn_in = {k: v for k, v in _L0_gnn_all.items() if k in ('W', 'a')}
    del _L0_gnn_all

    def _L1_gnn_setup():
        import jax, jax.numpy as jnp
        import numpy as np
        D_IN = 128
        D_HID = 256
        key = jax.random.key(seed)
        k1, k2, k3, k4, k5, k6 = jax.random.split(key, 6)
        x = jax.random.normal(k1, (8, 2048, D_IN), dtype=jnp.float32)
        adj = jax.random.uniform(k2, (8, 2048, 2048), dtype=jnp.float32)
        s1 = 1.0 / np.sqrt(D_IN)
        s2 = 1.0 / np.sqrt(D_HID)
        W1 = jax.random.uniform(k3, (D_IN, D_HID), dtype=jnp.float32, minval=-s1, maxval=s1)
        b1 = jax.random.uniform(k4, (D_HID,), dtype=jnp.float32, minval=-s1, maxval=s1)
        W2 = jax.random.uniform(k5, (D_HID, D_IN), dtype=jnp.float32, minval=-s2, maxval=s2)
        b2 = jax.random.uniform(k6, (D_IN,), dtype=jnp.float32, minval=-s2, maxval=s2)
        eps = jnp.zeros((1,), dtype=jnp.float32)
        return {'x': x, 'adj': adj, 'eps': eps, 'W1': W1, 'b1': b1, 'W2': W2, 'b2': b2}
    _L1_gnn_all = _L1_gnn_setup()
    _L1_gnn_in = {k: v for k, v in _L1_gnn_all.items() if k in ('eps', 'W1', 'b1', 'W2', 'b2')}
    del _L1_gnn_all

    def _L2_gnn_setup():
        import jax, jax.numpy as jnp
        import numpy as np
        key = jax.random.key(seed)
        k1, k2, k3, k4 = jax.random.split(key, 4)
        B, N, F_in, F_out = (8, 1024, 128, 128)
        x = jax.random.normal(k1, (B, N, F_in), dtype=jnp.float32)
        adj = jax.random.uniform(k2, (B, N, N), dtype=jnp.float32)
        stdv = 1.0 / np.sqrt(F_out)
        weight = jax.random.uniform(k3, (F_in, F_out), dtype=jnp.float32, minval=-stdv, maxval=stdv)
        bias = jax.random.uniform(k4, (F_out,), dtype=jnp.float32, minval=-stdv, maxval=stdv)
        return {'x': x, 'adj': adj, 'weight': weight, 'bias': bias}
    _L2_gnn_all = _L2_gnn_setup()
    _L2_gnn_in = {k: v for k, v in _L2_gnn_all.items() if k in ('weight', 'bias')}
    del _L2_gnn_all

    def _L3_gnn_setup():
        import jax, jax.numpy as jnp
        import numpy as np
        B, N, D, C, L = (64, 256, 128, 128, 5)
        EDGE_P = 0.02

        def _gru_cell(m, h, w_ih, w_hh, b_ih, b_hh):
            gi = m @ w_ih.T + b_ih
            gh = h @ w_hh.T + b_hh
            i_r, i_z, i_n = jnp.split(gi, 3, axis=-1)
            h_r, h_z, h_n = jnp.split(gh, 3, axis=-1)
            r = jax.nn.sigmoid(i_r + h_r)
            z = jax.nn.sigmoid(i_z + h_z)
            n = jnp.tanh(i_n + r * h_n)
            return (1.0 - z) * n + z * h
        key = jax.random.key(seed)
        ks = jax.random.split(key, 8)
        x = jax.random.normal(ks[0], (B, N, D), dtype=jnp.float32)
        adj = (jax.random.uniform(ks[1], (B, N, N)) < EDGE_P).astype(jnp.float32)
        mask = jnp.ones((B, N), dtype=jnp.float32)
        s = 1.0 / np.sqrt(C).astype(np.float32)
        weight = jax.random.uniform(ks[2], (L, C, C), minval=-s, maxval=s, dtype=jnp.float32)
        w_ih = jax.random.uniform(ks[3], (3 * C, C), minval=-s, maxval=s, dtype=jnp.float32)
        w_hh = jax.random.uniform(ks[4], (3 * C, C), minval=-s, maxval=s, dtype=jnp.float32)
        b_ih = jax.random.uniform(ks[5], (3 * C,), minval=-s, maxval=s, dtype=jnp.float32)
        b_hh = jax.random.uniform(ks[6], (3 * C,), minval=-s, maxval=s, dtype=jnp.float32)
        return dict(x=x, adj=adj, mask=mask, weight=weight, w_ih=w_ih, w_hh=w_hh, b_ih=b_ih, b_hh=b_hh)
    _L3_gnn_all = _L3_gnn_setup()
    _L3_gnn_in = {k: v for k, v in _L3_gnn_all.items() if k in ('weight', 'w_ih', 'w_hh', 'b_ih', 'b_hh')}
    del _L3_gnn_all
    return {'x': x, 'adj': adj, 'nodemask': nodemask, 'L0_gnn_W': _L0_gnn_in['W'], 'L0_gnn_a': _L0_gnn_in['a'], 'L1_gnn_eps': _L1_gnn_in['eps'], 'L1_gnn_W1': _L1_gnn_in['W1'], 'L1_gnn_b1': _L1_gnn_in['b1'], 'L1_gnn_W2': _L1_gnn_in['W2'], 'L1_gnn_b2': _L1_gnn_in['b2'], 'L2_gnn_weight': _L2_gnn_in['weight'], 'L2_gnn_bias': _L2_gnn_in['bias'], 'L3_gnn_weight': _L3_gnn_in['weight'], 'L3_gnn_w_ih': _L3_gnn_in['w_ih'], 'L3_gnn_w_hh': _L3_gnn_in['w_hh'], 'L3_gnn_b_ih': _L3_gnn_in['b_ih'], 'L3_gnn_b_hh': _L3_gnn_in['b_hh']}

def reference(x, adj, nodemask, L0_gnn_W, L0_gnn_a, L1_gnn_eps, L1_gnn_W1, L1_gnn_b1, L1_gnn_W2, L1_gnn_b2, L2_gnn_weight, L2_gnn_bias, L3_gnn_weight, L3_gnn_w_ih, L3_gnn_w_hh, L3_gnn_b_ih, L3_gnn_b_hh):
    import jax
    import jax.numpy as jnp

    def _L0_gnn_ref(x, adj, W, a):
        import jax, jax.numpy as jnp
        import numpy as np
        B, N, IN_DIM, OUT_DIM, H = (8, 512, 128, 128, 4)
        D = OUT_DIM // H
        NEG_INF = -9000000000000000.0
        LRELU_SLOPE = 0.2
        h = jnp.einsum('bni,io->bno', x, W).reshape(x.shape[0], x.shape[1], H, D)
        h = h.transpose(0, 2, 1, 3)
        a1, a2 = (a[:, :D], a[:, D:])
        e_i = jnp.einsum('bhnd,hd->bhn', h, a1)
        e_j = jnp.einsum('bhmd,hd->bhm', h, a2)
        e = e_i[:, :, :, None] + e_j[:, :, None, :]
        e = jnp.where(e > 0, e, LRELU_SLOPE * e)
        e = jnp.where(adj[:, None, :, :] > 0, e, NEG_INF)
        attn = jax.nn.softmax(e, axis=-1)
        out = jnp.einsum('bhnm,bhmd->bhnd', attn, h)
        out = out.transpose(0, 2, 1, 3).reshape(x.shape[0], x.shape[1], H * D)
        return out

    def _L1_gnn_ref(x, adj, eps, W1, b1, W2, b2):
        import jax, jax.numpy as jnp
        import numpy as np
        D_IN = 128
        D_HID = 256
        aggregated = jnp.einsum('bnm,bmd->bnd', adj, x)
        h = (1.0 + eps) * x + aggregated
        h = jax.nn.relu(h @ W1 + b1)
        return h @ W2 + b2

    def _L2_gnn_ref(x, adj, weight, bias):
        import jax, jax.numpy as jnp
        import numpy as np
        support = jnp.einsum('bni,io->bno', x, weight)
        out = jnp.einsum('bnm,bmo->bno', adj, support)
        return out + bias

    def _L3_gnn_ref(x, adj, mask, weight, w_ih, w_hh, b_ih, b_hh):
        import jax, jax.numpy as jnp
        import numpy as np
        B, N, D, C, L = (64, 256, 128, 128, 5)
        EDGE_P = 0.02

        def _gru_cell(m, h, w_ih, w_hh, b_ih, b_hh):
            gi = m @ w_ih.T + b_ih
            gh = h @ w_hh.T + b_hh
            i_r, i_z, i_n = jnp.split(gi, 3, axis=-1)
            h_r, h_z, h_n = jnp.split(gh, 3, axis=-1)
            r = jax.nn.sigmoid(i_r + h_r)
            z = jax.nn.sigmoid(i_z + h_z)
            n = jnp.tanh(i_n + r * h_n)
            return (1.0 - z) * n + z * h
        A = (adj != 0).astype(x.dtype)
        h = x
        for l in range(weight.shape[0]):
            m = jnp.einsum('bnd,de->bne', h, weight[l])
            agg = jnp.einsum('bij,bid->bjd', A, m)
            h = _gru_cell(agg, h, w_ih, w_hh, b_ih, b_hh)
        return h * mask[..., None]
    h = jnp.maximum(_layernorm(x, axis=-1), 0.0)
    x = x + _L0_gnn_ref(h, adj, L0_gnn_W, L0_gnn_a)
    h = jnp.maximum(_layernorm(x, axis=-1), 0.0)
    x = x + _L1_gnn_ref(h, adj, L1_gnn_eps, L1_gnn_W1, L1_gnn_b1, L1_gnn_W2, L1_gnn_b2)
    h = jnp.maximum(_layernorm(x, axis=-1), 0.0)
    x = x + _L2_gnn_ref(h, adj, L2_gnn_weight, L2_gnn_bias)
    h = jnp.maximum(_layernorm(x, axis=-1), 0.0)
    x = x + _L3_gnn_ref(h, adj, nodemask, L3_gnn_weight, L3_gnn_w_ih, L3_gnn_w_hh, L3_gnn_b_ih, L3_gnn_b_hh)
    return x

_drawn_inputs = setup_inputs


def setup_inputs(seed=0):
    import zlib

    import numpy as np

    out = dict(_drawn_inputs(seed))
    spreads = {}
    factors = {'L1_gnn_b1': 3.993, 'L3_gnn_b_hh': 3.335}
    for name, (base, spread) in spreads.items():
        noise = np.random.default_rng([zlib.crc32(name.encode()), seed]).standard_normal(out[name].shape)
        drawn = base * np.exp(spread * noise) if base else spread * noise
        out[name] = jnp.asarray(drawn.astype(out[name].dtype))
    for name, factor in factors.items():
        out[name] = (out[name] * factor).astype(out[name].dtype)
    return out
```

```python
from contextlib import ExitStack

import concourse.bass as bass
from concourse import mybir
from concourse.alu_op_type import AluOpType as ALU

ACT = mybir.ActivationFunctionType
AXIS = mybir.AxisListType
F32 = mybir.dt.float32
F16 = mybir.dt.float16
BF16 = mybir.dt.bfloat16
I32 = mybir.dt.int32

GRAPHS, NODES, DIM = 64, 128, 128
HEADS = 4
HEAD_DIM = DIM // HEADS
HIDDEN = 256
GRU_STEPS = 5
GATES = 3
GROUP = 4
COLS = GROUP * NODES
STREAMS = 2
PAIRS = GRAPHS // (GROUP * STREAMS)
BANKS = 4
SLOTS = STREAMS * GRU_STEPS
EPS = 1e-5
SLOPE = 0.2
MASKED = -(2.0 ** 100)
SCALE_EXP = 12


def mm(nc, out, lhsT, rhs, start=True, stop=True):
    return nc.tensor.matmul(out, lhsT, rhs, start=start, stop=stop)


def build(nc, io):
    with ExitStack() as ctx:
        def sb(name, shape, dt=F32):
            return ctx.enter_context(nc.sbuf_tensor(name, shape, dt))

        t = {}
        t["x"] = sb("x_all", [128, GRAPHS, DIM])
        t["edges"] = sb("edges", [128, GRAPHS, NODES], F16)
        t["h0T"] = sb("h0T", [128, GRAPHS, NODES])
        t["ident"] = sb("ident", [128, 128])
        t["ident16"] = sb("ident16", [128, 128], F16)
        t["identb"] = sb("identb", [128, 128], BF16)
        t["W0"] = sb("W0", [128, DIM])
        t["score_i"] = sb("score_i", [128, HEADS, 128])
        t["score_j"] = sb("score_j", [128, HEADS, 128])
        t["self_eye"] = sb("self_eye", [128, 128])
        t["W1"] = sb("W1", [128, HIDDEN])
        t["W2"] = sb("W2", [128, 2, DIM])
        t["b1"] = sb("b1", [128, 2])
        t["b2"] = sb("b2", [128, DIM])
        t["W3"] = sb("W3", [128, DIM])
        t["b3"] = sb("b3", [128, DIM])
        t["gru_w"] = sb("gru_w", [128, 2, GRU_STEPS + 1, GATES * DIM], F16)
        t["gates_b"] = sb("gates_b", [128, 8])
        t["mask"] = sb("mask", [128, GRAPHS])
        psum = ctx.enter_context(nc.psum_tensor("psum", [128, STREAMS, BANKS, 512], F32))
        prologue(nc, io, t, psum)
        first_layers(nc, io, t, psum)
        gru_layer(nc, io, t, psum)


B_R, B_Z, B_NZ, B_IN, B_HN, UNSCALE, N_UNSCALE, SCALE = range(8)


def prologue(nc, io, t, psum):
    with ExitStack() as ctx:
        def sb(name, shape, dt=F32):
            return ctx.enter_context(nc.sbuf_tensor(name, shape, dt))

        def sem(name):
            return ctx.enter_context(nc.semaphore(name))

        a1 = sb("a1", [128, DIM])
        a2 = sb("a2", [128, DIM])
        wa = sb("wa", [128, 2, DIM])
        was = sb("was", [128, 2, HEADS])
        eps = sb("eps", [128, 1])
        gw = sb("gw", [128, GRU_STEPS, DIM])
        wi = sb("wi", [128, GATES, DIM])
        wh = sb("wh", [128, GATES, DIM])
        gwT = sb("gwT", [128, GRU_STEPS, DIM])
        wiT = sb("wiT", [128, GATES * DIM])
        bi = sb("bi", [128, GATES])
        bh = sb("bh", [128, GATES])
        nm = sb("nm", [64, 128])
        gf = sb("gf", [128, GRU_STEPS + 1, GATES * DIM])
        top = sb("top", [128, 1])
        top1 = sb("top1", [1, 2])
        bits = sb("bits", [128, 4], I32)
        ones = sb("ones", [1, 128])
        loaded = sem("weights_loaded")
        made = sem("constants_made")
        turned = sem("weights_transposed")
        kept = sem("transposes_kept")
        fused = sem("gru_weights_fused")
        maxed = sem("row_max_kept")
        scale_step = sem("scale_pe")
        link = sem("vector_link")
        glink = sem("gpsimd_link")
        P = psum[:, :, :, :].rearrange("p s b c -> p (s b) c")

        loads = [
            (t["W0"][:, :], io["L0_gnn_W"][:, :]),
            (a1[:, :].rearrange("p (h d) -> p h d", h=HEADS), io["L0_gnn_a"][:, 0:HEAD_DIM].partition_broadcast(128)),
            (a2[:, :].rearrange("p (h d) -> p h d", h=HEADS), io["L0_gnn_a"][:, HEAD_DIM:2 * HEAD_DIM].partition_broadcast(128)),
            (gw[:, :, :], io["L3_gnn_weight"].rearrange("l d e -> d l e")),
            (wi[:, :, :], io["L3_gnn_w_ih"].rearrange("(t c) e -> c t e", t=GATES)),
            (wh[:, :, :], io["L3_gnn_w_hh"].rearrange("(t c) e -> c t e", t=GATES)),
            (eps[:, :], io["L1_gnn_eps"][:].partition_broadcast(128)),
            (t["W1"][:, :], io["L1_gnn_W1"][:, :]),
            (t["W2"][:, :, :], io["L1_gnn_W2"].rearrange("(t k) d -> k t d", t=2)),
            (t["b2"][:, :], io["L1_gnn_b2"][:].partition_broadcast(128)),
            (t["W3"][:, :], io["L2_gnn_weight"][:, :]),
            (t["b3"][:, :], io["L2_gnn_bias"][:].partition_broadcast(128)),
            (nm[:, :], io["nodemask"][:, :]),
        ]
        columns = [
            (t["b1"][:, :], io["L1_gnn_b1"].rearrange("(t p) -> p t", t=2)),
            (bi[:, :], io["L3_gnn_b_ih"].rearrange("(t p) -> p t", t=GATES)),
            (bh[:, :], io["L3_gnn_b_hh"].rearrange("(t p) -> p t", t=GATES)),
        ]
        all_loaded = 16 * (len(loads) + len(columns))
        block = ctx.enter_context(nc.Block())

        @block.sync
        def _(sp):
            for out, in_ in loads:
                sp.dma_start(out, in_).then_inc(loaded, 16)
            with nc.allow_non_contiguous_dma(reason="bias vectors of 256 or 384 numbers, one per partition"):
                for out, in_ in columns:
                    sp.dma_start(out, in_).then_inc(loaded, 16)

        @block.gpsimd
        def _(pool):
            for k, eye in enumerate((t["ident"], t["ident16"], t["identb"])):
                pool.memset(eye[:, :], 0.0).then_inc(glink, 1)
                pool.wait_ge(glink, k + 1)
                pool.affine_select(out=eye[:, :], in_=eye[:, :], compare_op=ALU.not_equal, fill=1.0, base=0,
                                   pattern=[[-1, 128]], channel_multiplier=1).then_inc(made, 1)
            pool.memset(ones[:, :], 1.0).then_inc(made, 1)

        @block.tensor
        def _(pe):
            pe.wait_ge(made, 4)
            pe.wait_ge(loaded, all_loaded)
            sources = [gw[:, l, :] for l in range(GRU_STEPS)] + [wi[:, k, :] for k in range(GATES)] + \
                      [wh[:, k, :] for k in range(GATES)]
            for k, src in enumerate(sources):
                nc.tensor.transpose(P[:, k // 4, k % 4 * 128:(k % 4 + 1) * 128], src, t["ident"][:, :])
            nc.tensor.transpose(P[:, 2, 384:384 + GRAPHS], nm[:, :], t["ident"][0:64, 0:64]).then_inc(turned, 1)
            pe.wait_ge(kept, 1)
            for l in range(GRU_STEPS):
                last = mm(nc, P[:, 3 + l, 0:GATES * DIM], gwT[:, l, :], wiT[:, :])
            last.then_inc(fused, 1)
            pe.wait_ge(maxed, 1)
            nc.tensor.transpose(P[0:1, 0, 0:128], top[:, :], t["ident"][:, :]).then_inc(scale_step, 1)
            pe.wait_ge(maxed, 2)
            mm(nc, P[:, 1, 0:1], ones[:, :], top1[:, 0:1]).then_inc(scale_step, 1)

        @block.vector
        def _(dve):
            done = [0]

            def linked(ins):
                done[0] += 1
                ins.then_inc(link, 1)
                dve.wait_ge(link, done[0])

            v = nc.vector
            gb = t["gates_b"]
            dve.wait_ge(loaded, all_loaded)
            dve.wait_ge(made, 4)
            for k, (a, dst) in enumerate(((a1, t["score_i"]), (a2, t["score_j"]))):
                linked(v.tensor_tensor(wa[:, k, :], t["W0"][:, :], a[:, :], ALU.mult))
                linked(v.tensor_reduce(was[:, k, :], wa[:, k, :].rearrange("p (h d) -> p h d", h=HEADS),
                                       AXIS.X, ALU.add))
                linked(v.tensor_copy(dst[:, :, :], was[:, k, :].unsqueeze(2).to_broadcast([128, HEADS, 128])))
            linked(v.tensor_scalar(eps[:, :], eps[:, :], 1.0, None, ALU.add))
            linked(v.tensor_scalar(t["self_eye"][:, :], t["ident"][:, :], eps[:, 0:1], None, ALU.mult))
            linked(v.tensor_tensor(gb[:, B_R:B_Z + 1], bi[:, 0:2], bh[:, 0:2], ALU.add))
            linked(v.tensor_scalar(gb[:, B_NZ:B_NZ + 1], gb[:, B_Z:B_Z + 1], -1.0, None, ALU.mult))
            linked(v.tensor_copy(gb[:, B_IN:B_IN + 1], bi[:, 2:3]))
            dve.wait_ge(turned, 1)
            v.tensor_copy(gwT[:, 0:4, :], P[:, 0, :].rearrange("p (l e) -> p l e", l=4))
            v.tensor_copy(gwT[:, 4, :], P[:, 1, 0:128])
            v.tensor_copy(wiT[:, :], P[:, 1, 128:512])
            v.tensor_copy(gf[:, GRU_STEPS, :], P[:, 2, 0:384])
            v.tensor_copy(t["mask"][:, :], P[:, 2, 384:384 + GRAPHS]).then_inc(kept, 1)
            dve.wait_ge(fused, 1)
            linked(v.tensor_copy(gf[:, 0:GRU_STEPS, :], P[:, 3:3 + GRU_STEPS, 0:GATES * DIM]))
            v.tensor_reduce(top[:, :], gf[:, :, :].rearrange("p l c -> p (l c)"), AXIS.X, ALU.max,
                            apply_absolute_value=True).then_inc(maxed, 1)
            dve.wait_ge(scale_step, 1)
            linked(v.tensor_reduce(top1[:, 1:2], P[0:1, 0, 0:128], AXIS.X, ALU.max))
            v.tensor_scalar(top1[:, 0:1], top1[:, 1:2], 2.0 ** -100, None, ALU.max).then_inc(maxed, 1)
            dve.wait_ge(scale_step, 2)
            linked(v.tensor_copy(bits[:, 0:1], P[:, 1, 0:1].bitcast(I32)))
            linked(v.tensor_scalar(bits[:, 1:2], bits[:, 0:1], 0x7F800000, None, ALU.bitwise_and))
            linked(v.tensor_scalar(bits[:, 2:3], bits[:, 1:2], -1.0, float((254 + SCALE_EXP) << 23),
                                   ALU.mult, ALU.add))
            linked(v.tensor_scalar(bits[:, 3:4], bits[:, 1:2], float(-(SCALE_EXP << 23)), None, ALU.add))
            linked(v.tensor_copy(gb[:, SCALE:SCALE + 1], bits[:, 2:3].bitcast(F32)))
            linked(v.tensor_copy(gb[:, UNSCALE:UNSCALE + 1], bits[:, 3:4].bitcast(F32)))
            linked(v.tensor_scalar(gb[:, N_UNSCALE:N_UNSCALE + 1], gb[:, UNSCALE:UNSCALE + 1], -1.0, None, ALU.mult))
            linked(v.tensor_scalar(gb[:, B_HN:B_HN + 1], bh[:, 2:3], gb[:, SCALE:SCALE + 1], None, ALU.mult))
            linked(v.tensor_scalar(t["gru_w"][:, 0, :, :], gf[:, :, :], gb[:, SCALE:SCALE + 1], None, ALU.mult))
            linked(v.scalar_tensor_tensor(t["gru_w"][:, 1, :, :], gf[:, :, :], gb[:, SCALE:SCALE + 1],
                                          t["gru_w"][:, 0, :, :], ALU.mult, ALU.subtract))


def first_layers(nc, io, t, psum):
    with ExitStack() as ctx:
        def pair(name, shape, dt=F32):
            return [ctx.enter_context(nc.sbuf_tensor(f"{name}{s}", shape, dt)) for s in range(STREAMS)]

        def sem(name):
            return ctx.enter_context(nc.semaphore(name))

        stats = pair("stats", [128, GROUP, 6])
        mean_var = pair("mean_var", [128, GROUP, 2])
        log_var = pair("log_var", [128, GROUP])
        rstd = pair("rstd", [128, GROUP])
        y = pair("y", [128, GROUP, DIM])
        hT = pair("hT", [128, GROUP, NODES])
        hW = pair("hW", [128, GROUP, HEADS, HEAD_DIM + 1])
        adj = pair("adj", [128, GROUP, NODES])
        adjT = pair("adjT", [128, GROUP, NODES])
        adjT1 = pair("adjT1", [128, GROUP, NODES])
        gone = pair("gone", [128, GROUP, NODES], BF16)
        prob = pair("prob", [128, GROUP, HEADS, NODES])
        probT = pair("probT", [128, GROUP, HEADS, NODES])
        top = pair("row_max", [128, GROUP, HEADS])
        rsum = pair("rsum", [128, GROUP, HEADS])
        att = pair("att", [128, GROUP, HEADS, HEAD_DIM])
        zT = pair("zT", [128, GROUP, NODES])
        hid = pair("hid", [128, 2, COLS])
        eps_col = ctx.enter_context(nc.sbuf_tensor("eps_col", [128, 1], F32))

        x_loaded = [sem(f"x_loaded{s}") for s in range(STREAMS)]
        adj_loaded = [sem(f"adj_loaded{s}") for s in range(STREAMS)]
        edges_ready = sem("edges_ready")
        passed = {e: sem(f"{e}_passed") for e in ("vector", "gpsimd")}
        eps_made = sem("eps_made")
        ones_made = sem("ones_made")
        stats_done = sem("stats_done")
        var_ready = sem("var_ready")
        log_done = sem("log_done")
        rstd_ready = sem("rstd_ready")
        y_ready = sem("y_ready")
        relu_done = sem("relu_done")
        yT_ready = sem("yT_ready")
        hT_ready = sem("hT_ready")
        adjT_psum = sem("adjT_psum")
        adjT_ready = sem("adjT_ready")
        adjT1_ready = sem("adjT1_ready")
        gone_ready = sem("gone_ready")
        hW_psum = sem("hW_psum")
        hW_ready = sem("hW_ready")
        score_ready = sem("score_ready")
        sloped = sem("sloped")
        lrelu_done = sem("lrelu_done")
        max_done = sem("max_done")
        shifted = sem("shifted")
        exp_done = sem("exp_done")
        probT_psum = sem("probT_psum")
        probT_act = sem("probT_act")
        probT_dve = sem("probT_dve")
        att_psum = sem("att_psum")
        rsum_done = sem("rsum_done")
        att_done = sem("att_done")
        x_attended = sem("x_attended")
        biased = sem("biased")
        z_psum = sem("z_psum")
        z_ready = sem("z_ready")
        hid_psum = sem("hid_psum")
        hid_act = sem("hid_act")
        hid_dve = sem("hid_dve")
        out_psum = sem("out_psum")
        x_added = sem("x_added")
        h0T_psum = sem("h0T_psum")
        h0T_kept = sem("h0T_kept")

        def nth(p, s, r=0, of=1):
            return p * (STREAMS * of) + (STREAMS * r + s + 1)

        def nth_graph(p, s, g):
            return p * (STREAMS * GROUP) + (GROUP * s + g + 1)

        def xs(p, s):
            return t["x"][:, bass.ds(p * (STREAMS * GROUP) + s * GROUP, GROUP), :]

        block = ctx.enter_context(nc.Block())

        def wait_apart(eng, engine, signal, count):
            eng.wait_ge(signal, count)
            eng.sem_inc(passed[engine], 1)

        @block.sync
        def _(sp):
            for s in range(STREAMS):
                sp.sem_inc(x_loaded[s], 16)
            with sp.Fori(0, PAIRS) as p:
                for s in range(STREAMS):
                    graphs = bass.ds(p * (STREAMS * GROUP) + s * GROUP, GROUP)
                    sp.wait_ge(x_loaded[s], 16 * p + 16)
                    sp.dma_start(xs(p, s), io["x"][graphs].rearrange("g n d -> n g d")).then_inc(x_loaded[s], 16)
                    sp.wait_ge(edges_ready, nth(p, s))
                    sp.wait_ge(adjT_psum, nth(p, s))
                    sp.dma_start(adj[s][:, :, :], io["adj"][graphs].rearrange("g n m -> n g m"))\
                        .then_inc(adj_loaded[s], 16)

        @block.gpsimd
        def _(pool):
            pool.memset(eps_col[:, :], EPS).then_inc(eps_made, 1)
            for s in range(STREAMS):
                pool.memset(hW[s][:, :, :, HEAD_DIM:], 1.0).then_inc(ones_made, 1)
            with pool.Fori(0, PAIRS) as p:
                for s in range(STREAMS):
                    pool.wait_ge(adjT_ready, nth(p, s))
                    pool.tensor_tensor(adjT1[s][:, :, :], adjT[s][:, :, :],
                                       t["self_eye"][:, :].unsqueeze(1).to_broadcast([128, GROUP, 128]), ALU.add)\
                        .then_inc(adjT1_ready, 1)
                for s in range(STREAMS):
                    for g in range(GROUP):
                        pool.wait_ge(max_done, nth_graph(p, s, g))
                        pool.tensor_tensor(prob[s][:, g, :, :], prob[s][:, g, :, :],
                                           top[s][:, g, :].unsqueeze(2).to_broadcast([128, HEADS, NODES]),
                                           ALU.subtract).then_inc(shifted, 1)
                for s in range(STREAMS):
                    pool.wait_ge(att_done, nth(p, s))
                    pool.tensor_tensor(xs(p, s), xs(p, s), att[s][:, :, :, :].rearrange("p g h d -> p g (h d)"),
                                       ALU.add).then_inc(x_attended, 1)
                for layer, bias in ((1, t["b2"]), (2, t["b3"])):
                    for s in range(STREAMS):
                        wait_apart(pool, "gpsimd", y_ready, nth(p, s, layer, 4))
                        pool.tensor_scalar(y[s][:, :, :], y[s][:, :, :], 0.0, None, ALU.max).then_inc(relu_done, 1)
                    for s in range(STREAMS):
                        pool.tensor_tensor(xs(p, s), xs(p, s),
                                           bias[:, :].unsqueeze(1).to_broadcast([128, GROUP, DIM]), ALU.add)\
                            .then_inc(biased, 1)

        @block.tensor
        def _(pe):
            pe.sem_inc(adjT_psum, STREAMS)
            pe.wait_ge(ones_made, STREAMS)
            with pe.Fori(0, PAIRS) as p:
                for s in range(STREAMS):
                    pe.wait_ge(adj_loaded[s], 16 * p + 16)
                    pe.wait_ge(h0T_kept, nth(p, s))
                    for g in range(GROUP):
                        last = nc.tensor.transpose(psum[:, s, 2, g * 128:(g + 1) * 128], adj[s][:, g, :], t["ident"][:, :])
                    last.then_inc(adjT_psum, 1)
                for s in range(STREAMS):
                    pe.wait_ge(y_ready, nth(p, s, 0, 4))
                    for g in range(GROUP):
                        last = nc.tensor.transpose(psum[:, s, 0, g * 128:(g + 1) * 128], y[s][:, g, :], t["ident"][:, :])
                    last.then_inc(yT_ready, 1)
                for s in range(STREAMS):
                    pe.wait_ge(hT_ready, nth(p, s))
                    for g in range(GROUP):
                        last = mm(nc, psum[:, s, 1, g * 128:(g + 1) * 128], hT[s][:, g, :], t["W0"][:, :])
                    last.then_inc(hW_psum, 1)
                for s in range(STREAMS):
                    for g in range(GROUP):
                        if g == 0:
                            pe.wait_ge(gone_ready, nth(p, s))
                        if g == 1:
                            pe.wait_ge(hW_ready, nth(p, s))
                        if g == 2:
                            pe.wait_ge(adjT_ready, nth(p, s))
                        bank = psum[:, s, g, :].rearrange("p (h m) -> p h m", h=HEADS)
                        mm(nc, bank, t["identb"][:, :],
                           gone[s][:, g, :].unsqueeze(1).to_broadcast([128, HEADS, NODES]), True, False)
                        mm(nc, bank, hT[s][:, g, :], t["score_i"][:, :, :], False, False)
                        for h in range(HEADS):
                            last = mm(nc, bank[:, h, :], t["score_j"][:, h, :], hT[s][:, g, :], False, h == HEADS - 1)
                        last.then_inc(score_ready, 1)
                for s in range(STREAMS):
                    for g in range(GROUP):
                        pe.wait_ge(exp_done, nth_graph(p, s, g))
                        for h in range(HEADS):
                            last = nc.tensor.transpose(psum[:, s, g, h * 128:(h + 1) * 128], prob[s][:, g, h, :],
                                                       t["ident"][:, :])
                        last.then_inc(probT_psum, 1)
                for s in range(STREAMS):
                    for g in range(GROUP):
                        if g % 2 == 0:
                            pe.wait_ge(probT_act, p * GROUP + (2 * s + g // 2 + 1))
                        else:
                            pe.wait_ge(probT_dve, p * GROUP + (2 * s + g // 2 + 1))
                        for h in range(HEADS):
                            last = mm(nc, psum[:, s, g, h * (HEAD_DIM + 1):(h + 1) * (HEAD_DIM + 1)],
                                      probT[s][:, g, h, :], hW[s][:, g, h, :])
                    last.then_inc(att_psum, 1)
                for layer in (1, 2):
                    for s in range(STREAMS):
                        near = adjT1[s] if layer == 1 else adjT[s]
                        if layer == 1:
                            pe.wait_ge(adjT1_ready, nth(p, s))
                        pe.wait_ge(relu_done, nth(p, s, layer - 1, 2))
                        for g in range(GROUP):
                            last = mm(nc, psum[:, s, 0, g * 128:(g + 1) * 128], y[s][:, g, :], near[:, g, :])
                        last.then_inc(z_psum, 1)
                    if layer == 1:
                        for s in range(STREAMS):
                            pe.wait_ge(z_ready, nth(p, s, 0, 2))
                            for k in range(2):
                                last = mm(nc, psum[:, s, 1 + k, :], t["W1"][:, k * 128:(k + 1) * 128],
                                          zT[s][:, :, :].rearrange("p g n -> p (g n)"))
                                last.then_inc(hid_psum, 1)
                        for s in range(STREAMS):
                            pe.wait_ge(hid_act, nth(p, s))
                            pe.wait_ge(hid_dve, nth(p, s))
                            for g in range(GROUP):
                                for k in range(2):
                                    last = mm(nc, psum[:, s, 3, g * 128:(g + 1) * 128],
                                              hid[s][:, k, g * 128:(g + 1) * 128], t["W2"][:, k, :], k == 0, k == 1)
                            last.then_inc(out_psum, 1)
                    else:
                        for s in range(STREAMS):
                            pe.wait_ge(z_ready, nth(p, s, 1, 2))
                            for g in range(GROUP):
                                last = mm(nc, psum[:, s, 1, g * 128:(g + 1) * 128], zT[s][:, g, :], t["W3"][:, :])
                            last.then_inc(out_psum, 1)
                for s in range(STREAMS):
                    pe.wait_ge(y_ready, nth(p, s, 3, 4))
                    for g in range(GROUP):
                        last = nc.tensor.transpose(psum[:, s, 2, g * 128:(g + 1) * 128], y[s][:, g, :], t["ident"][:, :])
                    last.then_inc(h0T_psum, 1)

        @block.scalar
        def _(act):
            def rstds(p, layer):
                for s in range(STREAMS):
                    act.wait_ge(var_ready, nth(p, s, layer, 4))
                    nc.scalar.activation(log_var[s][:, :], mean_var[s][:, :, 1], ACT.Ln, bias=eps_col[:, 0:1])\
                        .then_inc(log_done, 1)
                for s in range(STREAMS):
                    act.wait_ge(log_done, nth(p, s, layer, 4))
                    nc.scalar.activation(rstd[s][:, :], log_var[s][:, :], ACT.Exp, scale=-0.5).then_inc(rstd_ready, 1)

            act.sem_inc(h0T_kept, STREAMS)
            act.wait_ge(eps_made, 1)
            act.preload_act_table_set("natural_log_exp_and_others")
            with act.Fori(0, PAIRS) as p:
                rstds(p, 0)
                for s in range(STREAMS):
                    act.wait_ge(adjT_psum, nth(p, s) + STREAMS)
                    nc.scalar.copy(adjT[s][:, :, :].rearrange("p g n -> p (g n)"), psum[:, s, 2, :]).then_inc(adjT_ready, 1)
                for s in range(STREAMS):
                    act.wait_ge(yT_ready, nth(p, s))
                    nc.scalar.activation(hT[s][:, :, :].rearrange("p g n -> p (g n)"), psum[:, s, 0, :], ACT.Relu)\
                        .then_inc(hT_ready, 1)
                for s in range(STREAMS):
                    act.wait_ge(hW_psum, nth(p, s))
                    nc.scalar.copy(hW[s][:, :, :, 0:HEAD_DIM],
                                   psum[:, s, 1, :].rearrange("p (g h d) -> p g h d", g=GROUP, h=HEADS))\
                        .then_inc(hW_ready, 1)
                for s in range(STREAMS):
                    for g in range(GROUP):
                        act.wait_ge(score_ready, nth_graph(p, s, g))
                        nc.scalar.activation(prob[s][:, g, :, :].rearrange("p h m -> p (h m)"), psum[:, s, g, :],
                                             ACT.Copy, scale=SLOPE).then_inc(sloped, 1)
                for s in range(STREAMS):
                    for g in range(GROUP):
                        act.wait_ge(shifted, nth_graph(p, s, g))
                        nc.scalar.activation(prob[s][:, g, :, :], prob[s][:, g, :, :], ACT.Exp).then_inc(exp_done, 1)
                for s in range(STREAMS):
                    for g in range(0, GROUP, 2):
                        act.wait_ge(probT_psum, nth_graph(p, s, g))
                        nc.scalar.copy(probT[s][:, g, :, :].rearrange("p h n -> p (h n)"), psum[:, s, g, :])\
                            .then_inc(probT_act, 1)
                for layer in (1, 2):
                    rstds(p, layer)
                    for s in range(STREAMS):
                        act.wait_ge(z_psum, nth(p, s, layer - 1, 2))
                        nc.scalar.copy(zT[s][:, :, :].rearrange("p g n -> p (g n)"), psum[:, s, 0, :]).then_inc(z_ready, 1)
                    if layer == 1:
                        for s in range(STREAMS):
                            act.wait_ge(hid_psum, 2 * STREAMS * p + 2 * s + 1)
                            nc.scalar.activation(hid[s][:, 0, :], psum[:, s, 1, :], ACT.Relu, bias=t["b1"][:, 0:1])\
                                .then_inc(hid_act, 1)
                rstds(p, 3)
                for s in range(STREAMS):
                    act.wait_ge(h0T_psum, nth(p, s))
                    nc.scalar.activation(t["h0T"][:, bass.ds(p * (STREAMS * GROUP) + s * GROUP, GROUP), :],
                                         psum[:, s, 2, :].rearrange("p (g n) -> p g n", g=GROUP), ACT.Relu)\
                        .then_inc(h0T_kept, 1)

        @block.vector
        def _(dve):
            v = nc.vector

            def normalise(p, layer):
                for s in range(STREAMS):
                    if layer == 0:
                        wait_apart(dve, "vector", x_loaded[s], 16 * p + 32)
                    elif layer == 1:
                        wait_apart(dve, "vector", x_attended, nth(p, s))
                    else:
                        wait_apart(dve, "vector", x_added, nth(p, s, layer - 2, 2))
                    for g in range(GROUP):
                        last = v.bn_stats(stats[s][:, g, :], t["x"][:, p * (STREAMS * GROUP) + (s * GROUP + g), :])
                    last.then_inc(stats_done, 1)
                for s in range(STREAMS):
                    wait_apart(dve, "vector", stats_done, nth(p, s, layer, 4))
                    for g in range(GROUP):
                        last = v.bn_aggr(mean_var[s][:, g, :], stats[s][:, g, :])
                    last.then_inc(var_ready, 1)
                for s in range(STREAMS):
                    dve.wait_ge(rstd_ready, nth(p, s, layer, 4))
                    if layer == 0:
                        dve.wait_ge(h0T_kept, nth(p, s))
                    for g in range(GROUP):
                        last = v.tensor_scalar(y[s][:, g, :], t["x"][:, p * (STREAMS * GROUP) + (s * GROUP + g), :],
                                               mean_var[s][:, g, 0:1], rstd[s][:, g:g + 1], ALU.subtract, ALU.mult)
                    last.then_inc(y_ready, 1)

            dve.sem_inc(edges_ready, STREAMS)
            with dve.Fori(0, PAIRS) as p:
                for s in range(STREAMS):
                    dve.wait_ge(adj_loaded[s], 16 * p + 16)
                    v.tensor_scalar(gone[s][:, :, :], adj[s][:, :, :], 0.0, MASKED, ALU.is_le, ALU.mult)\
                        .then_inc(gone_ready, 1)
                    v.tensor_scalar(t["edges"][:, bass.ds(p * (STREAMS * GROUP) + s * GROUP, GROUP), :],
                                    adj[s][:, :, :], 0.0, None, ALU.not_equal).then_inc(edges_ready, 1)
                normalise(p, 0)
                for s in range(STREAMS):
                    for g in range(GROUP):
                        flat = prob[s][:, g, :, :].rearrange("p h m -> p (h m)")
                        dve.wait_ge(sloped, nth_graph(p, s, g))
                        v.tensor_tensor(flat, psum[:, s, g, :], flat, ALU.max).then_inc(lrelu_done, 1)
                        dve.wait_ge(lrelu_done, nth_graph(p, s, g))
                        v.tensor_reduce(top[s][:, g, :], prob[s][:, g, :, :], AXIS.X, ALU.max).then_inc(max_done, 1)
                for s in range(STREAMS):
                    for g in range(1, GROUP, 2):
                        dve.wait_ge(probT_psum, nth_graph(p, s, g))
                        v.tensor_copy(probT[s][:, g, :, :].rearrange("p h n -> p (h n)"), psum[:, s, g, :])\
                            .then_inc(probT_dve, 1)
                for s in range(STREAMS):
                    dve.wait_ge(att_psum, nth(p, s))
                    sums = psum[:, s, :, 0:HEADS * (HEAD_DIM + 1)].rearrange("p g (h d) -> p g h d", h=HEADS)
                    v.reciprocal(rsum[s][:, :, :], sums[:, :, :, HEAD_DIM]).then_inc(rsum_done, 1)
                    dve.wait_ge(rsum_done, nth(p, s))
                    v.tensor_tensor(att[s][:, :, :, :], sums[:, :, :, 0:HEAD_DIM],
                                    rsum[s][:, :, :].unsqueeze(3).to_broadcast([128, GROUP, HEADS, HEAD_DIM]),
                                    ALU.mult).then_inc(att_done, 1)
                for layer in (1, 2):
                    normalise(p, layer)
                    if layer == 1:
                        for s in range(STREAMS):
                            dve.wait_ge(hid_psum, 2 * STREAMS * p + 2 * s + 2)
                            v.tensor_scalar(hid[s][:, 1, :], psum[:, s, 2, :], t["b1"][:, 1:2], 0.0, ALU.add, ALU.max)\
                                .then_inc(hid_dve, 1)
                    for s in range(STREAMS):
                        dve.wait_ge(out_psum, nth(p, s, layer - 1, 2))
                        dve.wait_ge(biased, nth(p, s, layer - 1, 2))
                        bank = psum[:, s, 3 if layer == 1 else 1, :].rearrange("p (g d) -> p g d", g=GROUP)
                        v.tensor_tensor(xs(p, s), bank, xs(p, s), ALU.add).then_inc(x_added, 1)
                normalise(p, 3)


def gru_layer(nc, io, t, psum):
    with ExitStack() as ctx:
        def pair(name, shape, dt=F32):
            return [ctx.enter_context(nc.sbuf_tensor(f"{name}{s}", shape, dt)) for s in range(STREAMS)]

        def sem(name):
            return ctx.enter_context(nc.semaphore(name))

        h = pair("h", [128, COLS])
        hp = pair("h_parts", [128, 2, COLS], F16)
        hn = pair("h_nodes", [128, 2, GROUP, DIM], F16)
        tp = pair("t_parts", [128, 2, COLS], F16)
        r = pair("r", [128, COLS])
        z = pair("z", [128, COLS])
        zc = pair("zc", [128, COLS])
        zh = pair("zh", [128, COLS])
        cand = pair("cand", [128, COLS])
        new = pair("new", [128, COLS])
        out = pair("out", [128, GROUP, DIM])

        hi_ready = sem("hi_ready")
        lo_ready = sem("lo_ready")
        turned = sem("turned")
        nodes_ready = sem("nodes_ready")
        t_psum = sem("t_psum")
        t_hi = sem("t_hi")
        t_lo = sem("t_lo")
        r_psum = sem("r_psum")
        z_psum = sem("z_psum_gru")
        n_psum = sem("n_psum")
        r_ready = sem("r_ready")
        z_ready = sem("z_ready_gru")
        zc_ready = sem("zc_ready")
        zh_ready = sem("zh_ready")
        gated = sem("gated")
        summed = sem("summed")
        cand_ready = sem("cand_ready")
        mixed = sem("mixed")
        h_ready = sem("h_ready")
        back_psum = sem("back_psum")
        out_ready = sem("out_ready")
        stored = [sem(f"stored{s}") for s in range(STREAMS)]

        R, Z, N, T = range(BANKS)
        LAST = SLOTS - STREAMS
        gb = t["gates_b"]

        def col(i):
            return gb[:, i:i + 1]

        def at(p, k):
            return (p - 1, k + SLOTS) if k < 0 else (p + 1, k - SLOTS) if k >= SLOTS else (p, k)

        def nth(p, k):
            return p * SLOTS + (k + 1)

        def group_nth(p, s):
            return p * STREAMS + (s + 1)

        def group(p, s):
            return bass.ds(p * (STREAMS * GROUP) + s * GROUP, GROUP)

        def by_graph(x):
            return x.rearrange("p (g n) -> p g n", g=GROUP)

        def h_in(p, k):
            return t["h0T"][:, group(p, k), :] if k < STREAMS else by_graph(h[k % 2][:, :])

        def pairs(eng, pair_of_slots):
            pair_of_slots(0, False, True)
            with eng.Fori(1, PAIRS - 1) as p:
                pair_of_slots(p, True, True)
            pair_of_slots(PAIRS - 1, True, False)

        block = ctx.enter_context(nc.Block())

        @block.tensor
        def _(pe):
            def gate(bank, which, step, parts, terms, start=False, stop=False):
                for n, (w, m) in enumerate(terms):
                    last = mm(nc, bank, t["gru_w"][:, w, step, which * DIM:(which + 1) * DIM], parts[:, m, :],
                              start and n == 0, stop and n == len(terms) - 1)
                return last

            HI, LO = [(0, 0), (1, 0)], [(0, 1)]

            def back(p, s):
                pe.wait_ge(h_ready, nth(p, LAST + s))
                for g in range(GROUP):
                    last = nc.tensor.transpose(psum[:, s, N, g * 128:(g + 1) * 128], h[s][:, g * 128:(g + 1) * 128],
                                               t["ident"][:, :])
                last.then_inc(back_psum, 1)

            def slot(p, k, before):
                s, step = k % 2, k // 2
                bank = [psum[:, s, b, :] for b in range(BANKS)]
                turn = bank[T].bitcast(F16).rearrange("p (m g c) -> p m g c", m=2, g=GROUP)
                if k < STREAMS and before:
                    back(p - 1, s)
                pe.wait_ge(hi_ready, nth(p, k))
                for g in range(GROUP):
                    nc.tensor.transpose(turn[:, 0, g, :], hp[s][:, 0, g * 128:(g + 1) * 128], t["ident16"][:, :])
                gate(bank[R], 0, GRU_STEPS, hp[s], HI, start=True)
                pe.wait_ge(lo_ready, nth(p, k))
                for g in range(GROUP):
                    last = nc.tensor.transpose(turn[:, 1, g, :], hp[s][:, 1, g * 128:(g + 1) * 128], t["ident16"][:, :])
                last.then_inc(turned, 1)
                gate(bank[R], 0, GRU_STEPS, hp[s], LO)
                gate(bank[Z], 1, GRU_STEPS, hp[s], HI + LO, start=True)
                pe.wait_ge(nodes_ready, nth(p, k))
                for g in range(GROUP):
                    for m in range(2):
                        last = mm(nc, bank[T][:, g * 128:(g + 1) * 128], hn[s][:, m, g, :],
                                  t["edges"][:, p * (STREAMS * GROUP) + (s * GROUP + g), :], m == 0, m == 1)
                last.then_inc(t_psum, 1)
                if k < STREAMS and before:
                    pe.wait_ge(out_ready, group_nth(p - 1, s))
                gate(bank[N], 2, GRU_STEPS, hp[s], HI + LO, start=True, stop=True)
                pe.wait_ge(t_hi, nth(p, k))
                gate(bank[R], 0, step, tp[s], HI)
                gate(bank[Z], 1, step, tp[s], HI)
                pe.wait_ge(t_lo, nth(p, k))
                gate(bank[R], 0, step, tp[s], LO, stop=True).then_inc(r_psum, 1)
                gate(bank[Z], 1, step, tp[s], LO, stop=True).then_inc(z_psum, 1)
                gate(bank[T], 2, step, tp[s], HI + LO, start=True, stop=True).then_inc(n_psum, 1)

            def pair_of_slots(p, before, after):
                for k in range(SLOTS):
                    slot(p, k, before)

            pairs(pe, pair_of_slots)
            for s in range(STREAMS):
                back(PAIRS - 1, s)

        @block.scalar
        def _(act):
            def split_hi(p, k):
                if k >= STREAMS:
                    act.wait_ge(h_ready, nth(p, k - STREAMS))
                nc.scalar.copy(by_graph(hp[k % 2][:, 0, :]), h_in(p, k)).then_inc(hi_ready, 1)

            def candidate(p, k):
                act.wait_ge(summed, nth(p, k))
                nc.scalar.activation(cand[k % 2][:, :], new[k % 2][:, :], ACT.Tanh, bias=col(B_IN), scale=col(UNSCALE))\
                    .then_inc(cand_ready, 1)

            def pair_of_slots(p, before, after):
                for k in range(SLOTS):
                    s = k % 2
                    if k or before:
                        candidate(*at(p, k - 1))
                    act.wait_ge(t_psum, nth(p, k))
                    nc.scalar.copy(tp[s][:, 0, :], psum[:, s, T, :]).then_inc(t_hi, 1)
                    if k + 1 < SLOTS or after:
                        split_hi(*at(p, k + 1))
                    act.wait_ge(r_psum, nth(p, k))
                    nc.scalar.activation(r[s][:, :], psum[:, s, R, :], ACT.Sigmoid, bias=col(B_R), scale=col(UNSCALE))\
                        .then_inc(r_ready, 1)
                    act.wait_ge(z_psum, nth(p, k))
                    nc.scalar.activation(z[s][:, :], psum[:, s, Z, :], ACT.Sigmoid, bias=col(B_Z), scale=col(UNSCALE))\
                        .then_inc(z_ready, 1)
                    nc.scalar.activation(zc[s][:, :], psum[:, s, Z, :], ACT.Sigmoid, bias=col(B_NZ),
                                         scale=col(N_UNSCALE)).then_inc(zc_ready, 1)

            act.preload_act_table_set("sigmoid_and_others")
            split_hi(0, 0)
            pairs(act, pair_of_slots)
            candidate(PAIRS - 1, SLOTS - 1)

        @block.gpsimd
        def _(pool):
            with pool.Fori(0, PAIRS) as p:
                for k in range(SLOTS):
                    s = k % 2
                    pool.wait_ge(z_ready, nth(p, k))
                    pool.tensor_tensor(by_graph(zh[s][:, :]), by_graph(z[s][:, :]), h_in(p, k), ALU.mult)\
                        .then_inc(zh_ready, 1)

        @block.vector
        def _(dve):
            v = nc.vector

            def split_lo(p, k):
                dve.wait_ge(hi_ready, nth(p, k))
                v.tensor_tensor(by_graph(hp[k % 2][:, 1, :]), h_in(p, k), by_graph(hp[k % 2][:, 0, :]), ALU.subtract)\
                    .then_inc(lo_ready, 1)

            def add_input(p, k):
                s = k % 2
                dve.wait_ge(gated, nth(p, k))
                dve.wait_ge(n_psum, nth(p, k))
                v.tensor_tensor(new[s][:, :], psum[:, s, T, :], r[s][:, :], ALU.add).then_inc(summed, 1)

            def mix(p, k):
                s = k % 2
                dve.wait_ge(cand_ready, nth(p, k))
                dve.wait_ge(zc_ready, nth(p, k))
                v.tensor_tensor(cand[s][:, :], cand[s][:, :], zc[s][:, :], ALU.mult).then_inc(mixed, 1)

            def renew(p, k):
                s = k % 2
                dve.wait_ge(mixed, nth(p, k))
                dve.wait_ge(zh_ready, nth(p, k))
                v.tensor_tensor(h[s][:, :], cand[s][:, :], zh[s][:, :], ALU.add).then_inc(h_ready, 1)

            def finish(p, s):
                dve.wait_ge(back_psum, group_nth(p, s))
                dve.wait_ge(stored[s], 16 * p + 16)
                for g in range(GROUP):
                    graph = p * (STREAMS * GROUP) + (s * GROUP + g)
                    last = v.scalar_tensor_tensor(out[s][:, g, :], psum[:, s, N, g * 128:(g + 1) * 128],
                                                  t["mask"][:, bass.ds(graph, 1)], t["x"][:, graph, :],
                                                  ALU.mult, ALU.add)
                last.then_inc(out_ready, 1)

            def pair_of_slots(p, before, after):
                for k in range(SLOTS):
                    s = k % 2
                    tail = k > 0 or before
                    if tail:
                        add_input(*at(p, k - 1))
                    dve.wait_ge(turned, nth(p, k))
                    v.tensor_copy(hn[s][:, :, :, :].rearrange("p m g c -> p (m g c)"), psum[:, s, T, :].bitcast(F16))\
                        .then_inc(nodes_ready, 1)
                    if k < STREAMS and before:
                        finish(p - 1, s)
                    if tail:
                        mix(*at(p, k - 1))
                    dve.wait_ge(t_hi, nth(p, k))
                    v.tensor_tensor(tp[s][:, 1, :], psum[:, s, T, :], tp[s][:, 0, :], ALU.subtract).then_inc(t_lo, 1)
                    if tail:
                        renew(*at(p, k - 1))
                    if k + 1 < SLOTS or after:
                        split_lo(*at(p, k + 1))
                    dve.wait_ge(r_ready, nth(p, k))
                    v.scalar_tensor_tensor(r[s][:, :], psum[:, s, N, :], col(B_HN), r[s][:, :], ALU.add, ALU.mult)\
                        .then_inc(gated, 1)

            for s in range(STREAMS):
                dve.sem_inc(stored[s], 16)
            split_lo(0, 0)
            pairs(dve, pair_of_slots)
            add_input(PAIRS - 1, SLOTS - 1)
            mix(PAIRS - 1, SLOTS - 1)
            renew(PAIRS - 1, SLOTS - 1)
            for s in range(STREAMS):
                finish(PAIRS - 1, s)

        @block.sync
        def _(sp):
            with sp.Fori(0, PAIRS) as p:
                for s in range(STREAMS):
                    sp.wait_ge(out_ready, group_nth(p, s))
                    sp.dma_start(io["out"][group(p, s)].rearrange("g n d -> n g d"), out[s][:, :, :])\
                        .then_inc(stored[s], 16)
            for s in range(STREAMS):
                sp.wait_ge(stored[s], 16 * PAIRS + 16)


NAMES = ["x", "adj", "nodemask", "L0_gnn_W", "L0_gnn_a", "L1_gnn_eps", "L1_gnn_W1", "L1_gnn_b1", "L1_gnn_W2",
         "L1_gnn_b2", "L2_gnn_weight", "L2_gnn_bias", "L3_gnn_weight", "L3_gnn_w_ih", "L3_gnn_w_hh", "L3_gnn_b_ih",
         "L3_gnn_b_hh"]


def kernel(**inputs):
    import numpy as np
    import concourse.bacc as bacc
    from concourse.bass_utils import run_bass_kernel_spmd

    nc = bacc.Bacc("TRN2", target_bir_lowering=False, num_devices=1)
    arrays, io = {}, {}
    for name in NAMES:
        a = np.ascontiguousarray(inputs[name])
        arrays[f"in_{name}"] = a
        io[name] = nc.dram_tensor(f"in_{name}", a.shape, mybir.dt.from_np(a.dtype), kind="ExternalInput").ap()
    io["out"] = nc.dram_tensor("out_x", (GRAPHS, NODES, DIM), F32, kind="ExternalOutput").ap()
    build(nc, io)
    got = run_bass_kernel_spmd(nc, [arrays], core_ids=[0])
    return got.results[0]["out_x"]
```

```python
from contextlib import ExitStack

import concourse.bass as bass
from concourse import mybir
from concourse.alu_op_type import AluOpType as ALU

ACT = mybir.ActivationFunctionType
AXIS = mybir.AxisListType
F32 = mybir.dt.float32
F16 = mybir.dt.float16
BF16 = mybir.dt.bfloat16
I32 = mybir.dt.int32

GRAPHS, NODES, DIM = 64, 128, 128
HEADS = 4
HEAD_DIM = DIM // HEADS
HIDDEN = 256
GRU_STEPS = 5
GATES = 3
GROUP = 4
GROUPS = GRAPHS // GROUP
COLS = GROUP * NODES
STREAMS = 2
PAIRS = GROUPS // STREAMS
BANKS = 4
SLOTS = STREAMS * GRU_STEPS
LOOP_FROM = 2
EPS = 1e-5
SLOPE = 0.2
MASKED = -(2.0 ** 120)
LO_ROW = 32
SCALE_EXP = 12
SCORE_EXP = 7
LEAST = 2.0 ** -60


def mm(nc, out, lhsT, rhs, start=True, stop=True):
    return nc.tensor.matmul(out, lhsT, rhs, start=start, stop=stop)


def build(nc, io):
    with ExitStack() as ctx:
        def sb(name, shape, dt=F32):
            return ctx.enter_context(nc.sbuf_tensor(name, shape, dt))

        t = {}
        t["x"] = sb("x_all", [128, GRAPHS, DIM])
        t["edges"] = sb("edges", [128, GRAPHS, NODES], F16)
        t["h0T"] = sb("h0T", [128, GRAPHS, NODES])
        t["ident"] = sb("ident", [128, 128])
        t["ident16"] = sb("ident16", [128, 128], F16)
        t["identb"] = sb("identb", [128, 128], BF16)
        t["W0"] = sb("W0", [128, DIM])
        t["score_w"] = sb("score_w", [128, 128])
        t["pick_i"] = sb("pick_i", [128, HEADS, 128], F16)
        t["pick_j"] = sb("pick_j", [128, HEADS, 128], F16)
        t["self_eye"] = sb("self_eye", [128, 128])
        t["W1"] = sb("W1", [128, HIDDEN])
        t["W2"] = sb("W2", [128, 2, DIM])
        t["b1"] = sb("b1", [128, 2])
        t["b2"] = sb("b2", [128, DIM])
        t["W3"] = sb("W3", [128, DIM])
        t["b3"] = sb("b3", [128, DIM])
        t["gru_w"] = sb("gru_w", [128, 2, GRU_STEPS + 1, GATES * DIM], F16)
        t["gates_b"] = sb("gates_b", [128, 9])
        t["mask"] = sb("mask", [128, GRAPHS])
        psum = ctx.enter_context(nc.psum_tensor("psum", [128, STREAMS, BANKS, 512], F32))
        prologue(nc, io, t, psum)
        first_layers(nc, io, t, psum)
        gru_layer(nc, io, t, psum)


B_R, B_Z, B_NZ, B_IN, B_HN, UNSCALE, N_UNSCALE, SCALE, E_UNSCALE = range(9)


def prologue(nc, io, t, psum):
    with ExitStack() as ctx:
        def sb(name, shape, dt=F32):
            return ctx.enter_context(nc.sbuf_tensor(name, shape, dt))

        def sem(name):
            return ctx.enter_context(nc.semaphore(name))

        a1 = sb("a1", [128, DIM])
        a2 = sb("a2", [128, DIM])
        wa = sb("wa", [128, 2, DIM])
        was = sb("was", [128, 2, HEADS])
        eps = sb("eps", [128, 1])
        gw = sb("gw", [128, GRU_STEPS, DIM])
        wi = sb("wi", [128, GATES, DIM])
        wh = sb("wh", [128, GATES, DIM])
        gwT = sb("gwT", [128, GRU_STEPS, DIM])
        wiT = sb("wiT", [128, GATES * DIM])
        bi = sb("bi", [128, GATES])
        bh = sb("bh", [128, GATES])
        nm = sb("nm", [64, 128])
        gf = sb("gf", [128, GRU_STEPS + 1, GATES * DIM])
        top = sb("top", [128, 2])
        top1 = sb("top1", [1, 4])
        bits = sb("bits", [128, 2, 4], I32)
        ones = sb("ones", [1, 128])
        loaded = sem("weights_loaded")
        made = sem("constants_made")
        turned = sem("weights_transposed")
        kept = sem("transposes_kept")
        fused = sem("gru_weights_fused")
        maxed = sem("row_max_kept")
        scale_step = sem("scale_pe")
        link = sem("vector_link")
        glink = sem("gpsimd_link")
        P = psum[:, :, :, :].rearrange("p s b c -> p (s b) c")

        loads = [
            (t["W0"][:, :], io["L0_gnn_W"][:, :]),
            (a1[:, :].rearrange("p (h d) -> p h d", h=HEADS), io["L0_gnn_a"][:, 0:HEAD_DIM].partition_broadcast(128)),
            (a2[:, :].rearrange("p (h d) -> p h d", h=HEADS), io["L0_gnn_a"][:, HEAD_DIM:2 * HEAD_DIM].partition_broadcast(128)),
            (gw[:, :, :], io["L3_gnn_weight"].rearrange("l d e -> d l e")),
            (wi[:, :, :], io["L3_gnn_w_ih"].rearrange("(t c) e -> c t e", t=GATES)),
            (wh[:, :, :], io["L3_gnn_w_hh"].rearrange("(t c) e -> c t e", t=GATES)),
            (eps[:, :], io["L1_gnn_eps"][:].partition_broadcast(128)),
            (t["W1"][:, :], io["L1_gnn_W1"][:, :]),
            (t["W2"][:, :, :], io["L1_gnn_W2"].rearrange("(t k) d -> k t d", t=2)),
            (t["b2"][:, :], io["L1_gnn_b2"][:].partition_broadcast(128)),
            (t["W3"][:, :], io["L2_gnn_weight"][:, :]),
            (t["b3"][:, :], io["L2_gnn_bias"][:].partition_broadcast(128)),
            (nm[:, :], io["nodemask"][:, :]),
        ]
        columns = [
            (t["b1"][:, :], io["L1_gnn_b1"].rearrange("(t p) -> p t", t=2)),
            (bi[:, :], io["L3_gnn_b_ih"].rearrange("(t p) -> p t", t=GATES)),
            (bh[:, :], io["L3_gnn_b_hh"].rearrange("(t p) -> p t", t=GATES)),
        ]
        all_loaded = 16 * (len(loads) + len(columns))
        block = ctx.enter_context(nc.Block())

        @block.sync
        def _(sp):
            for out, in_ in loads:
                sp.dma_start(out, in_).then_inc(loaded, 16)
            with nc.allow_non_contiguous_dma(reason="bias vectors of 256 or 384 numbers, one per partition"):
                for out, in_ in columns:
                    sp.dma_start(out, in_).then_inc(loaded, 16)

        @block.gpsimd
        def _(pool):
            for k, eye in enumerate((t["ident"], t["ident16"], t["identb"])):
                pool.memset(eye[:, :], 0.0).then_inc(glink, 1)
                pool.wait_ge(glink, k + 1)
                pool.affine_select(out=eye[:, :], in_=eye[:, :], compare_op=ALU.not_equal, fill=1.0, base=0,
                                   pattern=[[-1, 128]], channel_multiplier=1).then_inc(made, 1)
            pool.memset(ones[:, :], 1.0).then_inc(made, 1)
            links = 3
            for pick, row in ((t["pick_i"], 0), (t["pick_j"], HEADS)):
                pool.memset(pick[:, :, :], 0.0).then_inc(glink, 1)
                links += 1
                for part in (0, LO_ROW):
                    pool.wait_ge(glink, links)
                    pool.affine_select(out=pick[:, :, :], in_=pick[:, :, :], compare_op=ALU.not_equal, fill=1.0,
                                       base=-(row + part), pattern=[[-1, HEADS], [0, 128]],
                                       channel_multiplier=1).then_inc(glink, 1)
                    links += 1

        @block.tensor
        def _(pe):
            pe.wait_ge(made, 4)
            pe.wait_ge(loaded, all_loaded)
            sources = [gw[:, l, :] for l in range(GRU_STEPS)] + [wi[:, k, :] for k in range(GATES)] + \
                      [wh[:, k, :] for k in range(GATES)]
            for k, src in enumerate(sources):
                nc.tensor.transpose(P[:, k // 4, k % 4 * 128:(k % 4 + 1) * 128], src, t["ident"][:, :])
            nc.tensor.transpose(P[:, 2, 384:384 + GRAPHS], nm[:, :], t["ident"][0:64, 0:64]).then_inc(turned, 1)
            pe.wait_ge(kept, 1)
            for l in range(GRU_STEPS):
                last = mm(nc, P[:, 3 + l, 0:GATES * DIM], gwT[:, l, :], wiT[:, :])
            last.then_inc(fused, 1)
            pe.wait_ge(maxed, 1)
            nc.tensor.transpose(P[0:1, 0, 0:128], top[:, 0:1], t["ident"][:, :])
            nc.tensor.transpose(P[0:1, 0, 128:256], top[:, 1:2], t["ident"][:, :]).then_inc(scale_step, 1)
            pe.wait_ge(maxed, 2)
            mm(nc, P[:, 1, 0:2], ones[:, :], top1[:, 0:2]).then_inc(scale_step, 1)

        @block.vector
        def _(dve):
            done = [0]

            def linked(ins):
                done[0] += 1
                ins.then_inc(link, 1)
                dve.wait_ge(link, done[0])

            v = nc.vector
            gb = t["gates_b"]
            dve.wait_ge(loaded, all_loaded)
            dve.wait_ge(made, 4)
            linked(v.memset(t["score_w"][:, :], 0.0))
            for k, a in enumerate((a1, a2)):
                linked(v.tensor_tensor(wa[:, k, :], t["W0"][:, :], a[:, :], ALU.mult))
                linked(v.tensor_reduce(was[:, k, :], wa[:, k, :].rearrange("p (h d) -> p h d", h=HEADS),
                                       AXIS.X, ALU.add))
            linked(v.tensor_scalar(eps[:, :], eps[:, :], 1.0, None, ALU.add))
            linked(v.tensor_scalar(t["self_eye"][:, :], t["ident"][:, :], eps[:, 0:1], None, ALU.mult))
            linked(v.tensor_tensor(gb[:, B_R:B_Z + 1], bi[:, 0:2], bh[:, 0:2], ALU.add))
            linked(v.tensor_scalar(gb[:, B_NZ:B_NZ + 1], gb[:, B_Z:B_Z + 1], -1.0, None, ALU.mult))
            linked(v.tensor_copy(gb[:, B_IN:B_IN + 1], bi[:, 2:3]))
            dve.wait_ge(turned, 1)
            v.tensor_copy(gwT[:, 0:4, :], P[:, 0, :].rearrange("p (l e) -> p l e", l=4))
            v.tensor_copy(gwT[:, 4, :], P[:, 1, 0:128])
            v.tensor_copy(wiT[:, :], P[:, 1, 128:512])
            v.tensor_copy(gf[:, GRU_STEPS, :], P[:, 2, 0:384])
            v.tensor_copy(t["mask"][:, :], P[:, 2, 384:384 + GRAPHS]).then_inc(kept, 1)
            dve.wait_ge(fused, 1)
            linked(v.tensor_copy(gf[:, 0:GRU_STEPS, :], P[:, 3:3 + GRU_STEPS, 0:GATES * DIM]))
            linked(v.tensor_reduce(top[:, 1:2], was[:, :, :].rearrange("p k h -> p (k h)"), AXIS.X, ALU.max,
                                   apply_absolute_value=True))
            v.tensor_reduce(top[:, 0:1], gf[:, :, :].rearrange("p l c -> p (l c)"), AXIS.X, ALU.max,
                            apply_absolute_value=True).then_inc(maxed, 1)
            dve.wait_ge(scale_step, 1)
            linked(v.tensor_reduce(top1[:, 2:4], P[0:1, 0, 0:256].rearrange("p (k c) -> p k c", k=2), AXIS.X, ALU.max))
            v.tensor_scalar(top1[:, 0:2], top1[:, 2:4], LEAST, None, ALU.max).then_inc(maxed, 1)
            dve.wait_ge(scale_step, 2)
            for k, (exp, scale, unscale) in enumerate(((SCALE_EXP, gb[:, SCALE:SCALE + 1], gb[:, UNSCALE:UNSCALE + 1]),
                                                       (SCORE_EXP, top[:, 0:1], gb[:, E_UNSCALE:E_UNSCALE + 1]))):
                b = bits[:, k, :]
                linked(v.tensor_copy(b[:, 0:1], P[:, 1, k:k + 1].bitcast(I32)))
                linked(v.tensor_scalar(b[:, 1:2], b[:, 0:1], 0x7F800000, None, ALU.bitwise_and))
                linked(v.tensor_scalar(b[:, 2:3], b[:, 1:2], -1.0, float((254 + exp) << 23), ALU.mult, ALU.add))
                linked(v.tensor_scalar(b[:, 3:4], b[:, 1:2], float(-(exp << 23)), None, ALU.add))
                linked(v.tensor_copy(scale, b[:, 2:3].bitcast(F32)))
                linked(v.tensor_copy(unscale, b[:, 3:4].bitcast(F32)))
            for row in (0, LO_ROW):
                linked(v.tensor_scalar(t["score_w"][:, row:row + 2 * HEADS], was[:, :, :].rearrange("p k h -> p (k h)"),
                                       top[:, 0:1], None, ALU.mult))
            linked(v.tensor_scalar(gb[:, N_UNSCALE:N_UNSCALE + 1], gb[:, UNSCALE:UNSCALE + 1], -1.0, None, ALU.mult))
            linked(v.tensor_scalar(gb[:, B_HN:B_HN + 1], bh[:, 2:3], gb[:, SCALE:SCALE + 1], None, ALU.mult))
            linked(v.tensor_scalar(t["gru_w"][:, 0, :, :], gf[:, :, :], gb[:, SCALE:SCALE + 1], None, ALU.mult))
            linked(v.scalar_tensor_tensor(t["gru_w"][:, 1, :, :], gf[:, :, :], gb[:, SCALE:SCALE + 1],
                                          t["gru_w"][:, 0, :, :], ALU.mult, ALU.subtract))


def first_layers(nc, io, t, psum):
    with ExitStack() as ctx:
        def one(name, shape, dt=F32):
            return ctx.enter_context(nc.sbuf_tensor(name, shape, dt))

        def two(name, shape, dt=F32):
            return [one(f"{name}{s}", shape, dt) for s in range(2)]

        def sem(name):
            return ctx.enter_context(nc.semaphore(name))

        LAYERS = range(4)
        stats = [one(f"stats{n}", [128, GROUP, 6]) for n in LAYERS]
        mean_var = [one(f"mean_var{n}", [128, GROUP, 2]) for n in LAYERS]
        log_var = [one(f"log_var{n}", [128, GROUP]) for n in LAYERS]
        rstd = [one(f"rstd{n}", [128, GROUP]) for n in LAYERS]
        shift = [one(f"shift{n}", [128, GROUP]) for n in LAYERS]
        y = [one(f"y{n}", [128, GROUP, DIM]) for n in LAYERS]
        hT = one("hT", [128, COLS])
        e_parts = two("e_parts", [128, COLS], F16)
        hW = two("hW", [128, GROUP, HEADS, HEAD_DIM + 1])
        adj = two("adj", [128, GROUP, NODES])
        adjT = two("adjT", [128, GROUP, NODES])
        adjT1 = two("adjT1", [128, GROUP, NODES])
        gone = two("gone", [128, GROUP, NODES], BF16)
        prob = one("prob", [128, GROUP, HEADS, NODES])
        probT = one("probT", [128, GROUP, HEADS, NODES])
        top = one("row_max", [128, GROUP, HEADS])
        rsum = one("rsum", [128, GROUP, HEADS])
        att = one("att", [128, GROUP, HEADS, HEAD_DIM])
        zT = [one(f"zT{n}", [128, GROUP, NODES]) for n in range(2)]
        hid = one("hid", [128, 2, COLS])
        eps_col = one("eps_col", [128, 1])

        x_loaded = [sem(f"x_loaded{s}") for s in range(2)]
        adj_loaded = [sem(f"adj_loaded{s}") for s in range(2)]
        constants = sem("constants")
        passed = {e: sem(f"{e}_passed") for e in ("vector", "scalar", "gpsimd")}
        stats_done = [sem(f"stats_done{n}") for n in LAYERS]
        var_ready = [sem(f"var_ready{n}") for n in LAYERS]
        log_done = [sem(f"log_done{n}") for n in LAYERS]
        rstd_ready = [sem(f"rstd_ready{n}") for n in LAYERS]
        shift_ready = [sem(f"shift_ready{n}") for n in LAYERS]
        y_ready = [sem(f"y_ready{n}") for n in LAYERS]
        gone_ready = sem("gone_ready")
        edges_ready = sem("edges_ready")
        yT_psum = sem("yT_psum")
        hT_ready = sem("hT_ready")
        e_psum = sem("e_psum")
        e_hi = sem("e_hi")
        e_lo = sem("e_lo")
        hW_psum = sem("hW_psum")
        hW_ready = sem("hW_ready")
        adjT_psum = sem("adjT_psum")
        adjT_ready = sem("adjT_ready")
        adjT1_ready = sem("adjT1_ready")
        score_ready = sem("score_ready")
        sloped = sem("sloped")
        lrelu_done = sem("lrelu_done")
        max_done = sem("max_done")
        shifted = sem("shifted")
        exp_done = sem("exp_done")
        probT_psum = sem("probT_psum")
        probT_act = sem("probT_act")
        probT_dve = sem("probT_dve")
        att_psum = sem("att_psum")
        rsum_done = sem("rsum_done")
        att_done = sem("att_done")
        x_attended = sem("x_attended")
        biased = [sem(f"biased{n}") for n in range(2)]
        z_psum = [sem(f"z_psum{n}") for n in range(2)]
        z_ready = [sem(f"z_ready{n}") for n in range(2)]
        out_psum = [sem(f"out_psum{n}") for n in range(2)]
        x_added = [sem(f"x_added{n}") for n in range(2)]
        hid_psum = [sem(f"hid_psum{k}") for k in range(2)]
        hid_ready = [sem(f"hid_ready{k}") for k in range(2)]
        h0T_psum = sem("h0T_psum")
        h0T_kept = sem("h0T_kept")

        B_LATE, B_TURN, B_HW, B_WIDE = 4, 5, 6, 7
        P = psum[:, :, :, :].rearrange("p s b c -> p (s b) c")
        BACKS = 4

        class Group:

            def __init__(self, p, q, back):
                self.p, self.q, self.back = p, q, back
                self.number = p * 2 + (q - back)
                self.odd = (q - back) % 2
                self.count = p * 2 + (q - back + 1)
                self.loads = p * 16 + 16 * ((q - back) // 2 + 1)
                self.exists = not isinstance(p, int) or 0 <= self.number < GROUPS
                self.all = bass.ds(self.number * GROUP, GROUP)

            def graph(self, g):
                return self.number * GROUP + g

            def graph_count(self, g):
                return self.number * GROUP + (g + 1)

            def half_count(self, g):
                return self.number * 2 + (g // 2 + 1)

            def before(self, n):
                return Group(self.p, self.q, self.back + n)

        def xs(group):
            return t["x"][:, group.all, :]

        def flat(x):
            return x.rearrange("p g n -> p (g n)")

        def slots(eng, slot):
            def one_slot(p, q):
                def at(back):
                    group = Group(p, q, back)
                    return group if group.exists else None
                slot(at)

            for p in range(LOOP_FROM):
                for q in range(2):
                    one_slot(p, q)
            with eng.Fori(LOOP_FROM, GROUPS // 2) as p:
                for q in range(2):
                    one_slot(p, q)
            for q in range(BACKS - 1):
                one_slot(GROUPS // 2, q)

        def wait_users(eng, *users):
            for signal, group in users:
                if group.exists:
                    eng.wait_ge(signal, group.count)
                    return

        def apart(eng, name):
            def wait_apart(signal, count):
                eng.wait_ge(signal, count)
                eng.sem_inc(passed[name], 1)
            return wait_apart

        block = ctx.enter_context(nc.Block())

        @block.sync
        def _(sp):
            def load(p, first):
                for q in range(2):
                    group = Group(p, q, 0)
                    if not first:
                        sp.wait_ge(x_loaded[q], 16 * p)
                    sp.dma_start(xs(group), io["x"][group.all].rearrange("g n d -> n g d")).then_inc(x_loaded[q], 16)
                    if not first:
                        sp.wait_ge(adjT_psum, group.before(2).count)
                        sp.wait_ge(gone_ready, group.before(2).count)
                        sp.wait_ge(edges_ready, group.before(2).count)
                    sp.dma_start(adj[q][:, :, :], io["adj"][group.all].rearrange("g n m -> n g m"))\
                        .then_inc(adj_loaded[q], 16)

            load(0, True)
            with sp.Fori(1, GROUPS // 2) as p:
                load(p, False)

        @block.gpsimd
        def _(pool):
            wait_apart = apart(pool, "gpsimd")

            def add_self(group):
                pool.wait_ge(adjT_ready, group.count)
                if group.before(2).exists:
                    pool.wait_ge(z_psum[0], group.before(2).count)
                pool.tensor_tensor(adjT1[group.odd][:, :, :], adjT[group.odd][:, :, :],
                                   t["self_eye"][:, :].unsqueeze(1).to_broadcast([128, GROUP, 128]), ALU.add)\
                    .then_inc(adjT1_ready, 1)

            def bias(group, n, b):
                wait_apart(y_ready[n + 1], group.count)
                pool.tensor_tensor(xs(group), xs(group), b[:, :].unsqueeze(1).to_broadcast([128, GROUP, DIM]), ALU.add)\
                    .then_inc(biased[n], 1)

            def less_max(group, g):
                pool.wait_ge(max_done, group.graph_count(g))
                pool.tensor_tensor(prob[:, g, :, :], prob[:, g, :, :],
                                   top[:, g, :].unsqueeze(2).to_broadcast([128, HEADS, NODES]),
                                   ALU.subtract).then_inc(shifted, 1)

            def add_attended(group):
                wait_apart(att_done, group.count)
                pool.tensor_tensor(xs(group), xs(group), att[:, :, :, :].rearrange("p g h d -> p g (h d)"), ALU.add)\
                    .then_inc(x_attended, 1)

            def slot(at):
                if at(1):
                    add_self(at(1))
                if at(2):
                    bias(at(2), 1, t["b3"])
                if at(0):
                    less_max(at(0), 0)
                    less_max(at(0), 1)
                    less_max(at(0), 2)
                if at(1):
                    bias(at(1), 0, t["b2"])
                if at(0):
                    less_max(at(0), 3)
                    add_attended(at(0))

            pool.memset(eps_col[:, :], EPS).then_inc(constants, 1)
            for s in range(2):
                pool.memset(hW[s][:, :, :, HEAD_DIM:], 1.0).then_inc(constants, 1)
            pool.wait_ge(constants, 3)
            slots(pool, slot)

        @block.tensor
        def _(pe):
            def turn(bank, src):
                for g in range(GROUP):
                    last = nc.tensor.transpose(P[:, bank, g * 128:(g + 1) * 128], src[:, g, :], t["ident"][:, :])
                return last

            def turn_y0(group):
                pe.wait_ge(y_ready[0], group.count)
                wait_users(pe, (hid_ready[1], group.before(2)), (hT_ready, group.before(1)))
                turn(B_TURN, y[0]).then_inc(yT_psum, 1)

            def score_terms(group):
                pe.wait_ge(hT_ready, group.count)
                wait_users(pe, (hid_ready[0], group.before(2)), (e_lo, group.before(1)))
                mm(nc, P[:, B_WIDE, :], t["score_w"][:, :], hT[:, :]).then_inc(e_psum, 1)

            def project(group):
                pe.wait_ge(hT_ready, group.count)
                wait_users(pe, (hW_ready, group.before(1)))
                for g in range(GROUP):
                    last = mm(nc, P[:, B_HW, g * 128:(g + 1) * 128], hT[:, g * 128:(g + 1) * 128], t["W0"][:, :])
                last.then_inc(hW_psum, 1)

            def turn_adj(group):
                pe.wait_ge(adj_loaded[group.odd], group.loads)
                wait_users(pe, (hT_ready, group.before(-1)), (hid_ready[1], group.before(1)))
                turn(B_TURN, adj[group.odd]).then_inc(adjT_psum, 1)

            def scores(group, g):
                pe.wait_ge(gone_ready, group.count)
                pe.wait_ge(e_hi, group.count)
                pe.wait_ge(e_lo, group.count)
                wait_users(pe, (att_done, group.before(1)))
                bank = P[:, g, :].rearrange("p (h m) -> p h m", h=HEADS)
                e = e_parts[group.odd][:, g * 128:(g + 1) * 128]
                mm(nc, bank, t["identb"][:, :],
                   gone[group.odd][:, g, :].unsqueeze(1).to_broadcast([128, HEADS, NODES]), True, False)
                mm(nc, bank, e, t["pick_i"][:, :, :], False, False)
                for h in range(HEADS):
                    last = mm(nc, bank[:, h, :], t["pick_j"][:, h, :], e, False, h == HEADS - 1)
                last.then_inc(score_ready, 1)

            def turn_prob(group, g):
                pe.wait_ge(exp_done, group.graph_count(g))
                for h in range(HEADS):
                    last = nc.tensor.transpose(P[:, g, h * 128:(h + 1) * 128], prob[:, g, h, :], t["ident"][:, :])
                last.then_inc(probT_psum, 1)

            def attend(group, g):
                pe.wait_ge(probT_dve if g % 2 else probT_act, group.half_count(g))
                pe.wait_ge(hW_ready, group.count)
                for h in range(HEADS):
                    last = mm(nc, P[:, g, h * (HEAD_DIM + 1):(h + 1) * (HEAD_DIM + 1)], probT[:, g, h, :],
                              hW[group.odd][:, g, h, :])
                if g == GROUP - 1:
                    last.then_inc(att_psum, 1)

            def neighbours(group, n, bank, near, signal):
                pe.wait_ge(y_ready[n + 1], group.count)
                pe.wait_ge(signal, group.count)
                if n == 1:
                    wait_users(pe, (h0T_kept, group.before(1)))
                for g in range(GROUP):
                    last = mm(nc, P[:, bank, g * 128:(g + 1) * 128], y[n + 1][:, g, :], near[:, g, :])
                last.then_inc(z_psum[n], 1)

            def hidden(group, k, bank):
                pe.wait_ge(z_ready[0], group.count)
                if k == 0:
                    wait_users(pe, (x_added[1], group.before(1)), (e_lo, group.before(-1)))
                mm(nc, P[:, bank, :], t["W1"][:, k * 128:(k + 1) * 128], flat(zT[0][:, :, :]))\
                    .then_inc(hid_psum[k], 1)

            def out_0(group):
                pe.wait_ge(hid_ready[0], group.count)
                pe.wait_ge(hid_ready[1], group.count)
                wait_users(pe, (z_ready[1], group.before(1)))
                for g in range(GROUP):
                    for k in range(2):
                        last = mm(nc, P[:, B_LATE, g * 128:(g + 1) * 128], hid[:, k, g * 128:(g + 1) * 128],
                                  t["W2"][:, k, :], k == 0, k == 1)
                last.then_inc(out_psum[0], 1)

            def out_1(group):
                pe.wait_ge(z_ready[1], group.count)
                wait_users(pe, (e_lo, group.before(-2)))
                for g in range(GROUP):
                    last = mm(nc, P[:, B_WIDE, g * 128:(g + 1) * 128], zT[1][:, g, :], t["W3"][:, :])
                last.then_inc(out_psum[1], 1)

            def turn_y3(group):
                pe.wait_ge(y_ready[3], group.count)
                wait_users(pe, (x_added[0], group.before(-1)))
                turn(B_LATE, y[3]).then_inc(h0T_psum, 1)

            def slot(at):
                if at(1):
                    turn_prob(at(1), 2)
                if at(2):
                    out_0(at(2))
                if at(0):
                    turn_y0(at(0))
                if at(1):
                    turn_prob(at(1), 3)
                    for g in range(GROUP):
                        attend(at(1), g)
                if at(0):
                    score_terms(at(0))
                if at(1):
                    turn_adj(at(1))
                if at(3):
                    turn_y3(at(3))
                if at(0):
                    scores(at(0), 0)
                    scores(at(0), 1)
                    scores(at(0), 2)
                if at(2):
                    neighbours(at(2), 1, B_LATE, adjT[at(2).odd], adjT_ready)
                if at(0):
                    scores(at(0), 3)
                    project(at(0))
                if at(2):
                    out_1(at(2))
                if at(1):
                    neighbours(at(1), 0, B_TURN, adjT1[at(1).odd], adjT1_ready)
                if at(0):
                    turn_prob(at(0), 0)
                if at(1):
                    hidden(at(1), 0, B_WIDE)
                    hidden(at(1), 1, B_TURN)
                if at(0):
                    turn_prob(at(0), 1)

            pe.wait_ge(constants, 3)
            slots(pe, slot)

        @block.scalar
        def _(act):
            a = nc.scalar
            wait_apart = apart(act, "scalar")

            def rstd_of(group, n):
                act.wait_ge(var_ready[n], group.count)
                a.activation(log_var[n][:, :], mean_var[n][:, :, 1], ACT.Ln, bias=eps_col[:, 0:1]).then_inc(log_done[n], 1)
                act.wait_ge(log_done[n], group.count)
                a.activation(rstd[n][:, :], log_var[n][:, :], ACT.Exp, scale=-0.5).then_inc(rstd_ready[n], 1)

            def normalise(group, n):
                wait_apart(shift_ready[n], group.count)
                for g in range(GROUP):
                    last = a.activation(y[n][:, g, :], t["x"][:, group.graph(g), :], ACT.Relu,
                                        bias=shift[n][:, g:g + 1], scale=rstd[n][:, g:g + 1])
                last.then_inc(y_ready[n], 1)

            def keep_hT(group):
                act.wait_ge(yT_psum, group.count)
                if group.before(1).exists:
                    act.wait_ge(e_psum, group.before(1).count)
                    act.wait_ge(hW_psum, group.before(1).count)
                a.activation(hT[:, :], P[:, B_TURN, :], ACT.Relu).then_inc(hT_ready, 1)

            def keep_e(group):
                act.wait_ge(e_psum, group.count)
                if group.before(2).exists:
                    act.wait_ge(score_ready, group.before(2).graph_count(GROUP - 1))
                a.copy(e_parts[group.odd][:, :], P[:, B_WIDE, :]).then_inc(e_hi, 1)

            def keep_hW(group):
                act.wait_ge(hW_psum, group.count)
                if group.before(2).exists:
                    act.wait_ge(att_psum, group.before(2).count)
                a.copy(hW[group.odd][:, :, :, 0:HEAD_DIM],
                       P[:, B_HW, :].rearrange("p (g h d) -> p g h d", g=GROUP, h=HEADS)).then_inc(hW_ready, 1)

            def keep_adjT(group):
                act.wait_ge(adjT_psum, group.count)
                if group.before(2).exists:
                    act.wait_ge(z_psum[1], group.before(2).count)
                a.copy(flat(adjT[group.odd][:, :, :]), P[:, B_TURN, :]).then_inc(adjT_ready, 1)

            def slope(group, g):
                act.wait_ge(score_ready, group.graph_count(g))
                a.activation(prob[:, g, :, :].rearrange("p h m -> p (h m)"), P[:, g, :], ACT.Copy, scale=SLOPE)\
                    .then_inc(sloped, 1)

            def exponential(group, g):
                act.wait_ge(shifted, group.graph_count(g))
                a.activation(prob[:, g, :, :], prob[:, g, :, :], ACT.Exp, scale=t["gates_b"][:, E_UNSCALE:E_UNSCALE + 1])\
                    .then_inc(exp_done, 1)

            def keep_probT(group, g):
                act.wait_ge(probT_psum, group.graph_count(g))
                a.copy(probT[:, g, :, :].rearrange("p h n -> p (h n)"), P[:, g, :]).then_inc(probT_act, 1)

            def keep_z(group, n, bank):
                act.wait_ge(z_psum[n], group.count)
                a.copy(flat(zT[n][:, :, :]), P[:, bank, :]).then_inc(z_ready[n], 1)

            def keep_hidden(group, k, bank):
                act.wait_ge(hid_psum[k], group.count)
                a.activation(hid[:, k, :], P[:, bank, :], ACT.Relu, bias=t["b1"][:, k:k + 1]).then_inc(hid_ready[k], 1)

            def slot(at):
                if at(1):
                    exponential(at(1), 1)
                    exponential(at(1), 2)
                if at(2):
                    keep_hidden(at(2), 0, B_WIDE)
                    keep_hidden(at(2), 1, B_TURN)
                if at(0):
                    rstd_of(at(0), 0)
                if at(1):
                    keep_hW(at(1))
                if at(3):
                    rstd_of(at(3), 3)
                if at(1):
                    exponential(at(1), 3)
                    keep_probT(at(1), 0)
                    keep_probT(at(1), 2)
                if at(0):
                    keep_hT(at(0))
                if at(3):
                    normalise(at(3), 3)
                if at(2):
                    rstd_of(at(2), 2)
                if at(0):
                    keep_e(at(0))
                if at(1):
                    keep_adjT(at(1))
                if at(2):
                    normalise(at(2), 2)
                if at(0):
                    slope(at(0), 0)
                    slope(at(0), 1)
                if at(1):
                    rstd_of(at(1), 1)
                if at(0):
                    slope(at(0), 2)
                if at(2):
                    keep_z(at(2), 1, B_LATE)
                if at(1):
                    normalise(at(1), 1)
                if at(0):
                    slope(at(0), 3)
                    exponential(at(0), 0)
                if at(1):
                    keep_z(at(1), 0, B_TURN)

            act.preload_act_table_set("natural_log_exp_and_others")
            act.wait_ge(constants, 3)
            slots(act, slot)

        @block.vector
        def _(dve):
            v = nc.vector
            wait_apart = apart(dve, "vector")

            def moments(group, n, signal, count):
                wait_apart(signal, count)
                for g in range(GROUP):
                    last = v.bn_stats(stats[n][:, g, :], t["x"][:, group.graph(g), :])
                last.then_inc(stats_done[n], 1)
                wait_apart(stats_done[n], group.count)
                for g in range(GROUP):
                    last = v.bn_aggr(mean_var[n][:, g, :], stats[n][:, g, :])
                last.then_inc(var_ready[n], 1)

            def shift_of(group, n):
                dve.wait_ge(rstd_ready[n], group.count)
                v.scalar_tensor_tensor(shift[n][:, :], mean_var[n][:, :, 0], -1.0, rstd[n][:, :], ALU.mult, ALU.mult)\
                    .then_inc(shift_ready[n], 1)

            def normalise_0(group):
                dve.wait_ge(rstd_ready[0], group.count)
                if group.before(1).exists:
                    dve.wait_ge(yT_psum, group.before(1).count)
                for g in range(GROUP):
                    last = v.tensor_scalar(y[0][:, g, :], t["x"][:, group.graph(g), :],
                                           mean_var[0][:, g, 0:1], rstd[0][:, g:g + 1], ALU.subtract, ALU.mult)
                last.then_inc(y_ready[0], 1)

            def find_gone(group):
                dve.wait_ge(adj_loaded[group.odd], group.loads)
                if group.before(2).exists:
                    dve.wait_ge(score_ready, group.before(2).graph_count(GROUP - 1))
                v.tensor_scalar(gone[group.odd][:, :, :], adj[group.odd][:, :, :], 0.0, MASKED, ALU.is_le, ALU.mult)\
                    .then_inc(gone_ready, 1)

            def find_edges(group):
                wait_apart(adj_loaded[group.odd], group.loads)
                v.tensor_scalar(t["edges"][:, group.all, :], adj[group.odd][:, :, :], 0.0, None, ALU.not_equal)\
                    .then_inc(edges_ready, 1)

            def keep_e_lo(group):
                dve.wait_ge(e_hi, group.count)
                v.tensor_tensor(e_parts[group.odd][LO_ROW:2 * LO_ROW, :], P[LO_ROW:2 * LO_ROW, B_WIDE, :],
                                e_parts[group.odd][LO_ROW:2 * LO_ROW, :], ALU.subtract).then_inc(e_lo, 1)

            def leaky(group, g):
                row = prob[:, g, :, :].rearrange("p h m -> p (h m)")
                dve.wait_ge(sloped, group.graph_count(g))
                v.tensor_tensor(row, P[:, g, :], row, ALU.max).then_inc(lrelu_done, 1)

            def row_max(group, g):
                dve.wait_ge(lrelu_done, group.graph_count(g))
                v.tensor_reduce(top[:, g, :], prob[:, g, :, :], AXIS.X, ALU.max).then_inc(max_done, 1)

            def keep_probT(group, g):
                dve.wait_ge(probT_psum, group.graph_count(g))
                v.tensor_copy(probT[:, g, :, :].rearrange("p h n -> p (h n)"), P[:, g, :]).then_inc(probT_dve, 1)

            def divide(group):
                dve.wait_ge(att_psum, group.count)
                sums = P[:, 0:GROUP, 0:HEADS * (HEAD_DIM + 1)].rearrange("p g (h d) -> p g h d", h=HEADS)
                v.reciprocal(rsum[:, :, :], sums[:, :, :, HEAD_DIM]).then_inc(rsum_done, 1)
                dve.wait_ge(rsum_done, group.count)
                v.tensor_tensor(att[:, :, :, :], sums[:, :, :, 0:HEAD_DIM],
                                rsum[:, :, :].unsqueeze(3).to_broadcast([128, GROUP, HEADS, HEAD_DIM]),
                                ALU.mult).then_inc(att_done, 1)

            def add_out(group, n, bank):
                dve.wait_ge(out_psum[n], group.count)
                dve.wait_ge(biased[n], group.count)
                v.tensor_tensor(xs(group), P[:, bank, :].rearrange("p (g d) -> p g d", g=GROUP), xs(group), ALU.add)\
                    .then_inc(x_added[n], 1)

            def keep_h0T(group):
                dve.wait_ge(h0T_psum, group.count)
                v.tensor_copy(t["h0T"][:, group.all, :], P[:, B_LATE, :].rearrange("p (g n) -> p g n", g=GROUP))\
                    .then_inc(h0T_kept, 1)

            def slot(at):
                if at(1):
                    row_max(at(1), 2)
                if at(3):
                    add_out(at(3), 1, B_WIDE)
                if at(1):
                    leaky(at(1), 3)
                if at(0):
                    moments(at(0), 0, x_loaded[at(0).odd], at(0).loads)
                if at(1):
                    row_max(at(1), 3)
                if at(3):
                    moments(at(3), 3, x_added[1], at(3).count)
                if at(0):
                    normalise_0(at(0))
                if at(3):
                    shift_of(at(3), 3)
                if at(1):
                    keep_probT(at(1), 1)
                if at(2):
                    add_out(at(2), 0, B_LATE)
                if at(1):
                    keep_probT(at(1), 3)
                if at(2):
                    moments(at(2), 2, x_added[0], at(2).count)
                if at(1):
                    divide(at(1))
                if at(2):
                    shift_of(at(2), 2)
                if at(0):
                    find_gone(at(0))
                    find_edges(at(0))
                    keep_e_lo(at(0))
                if at(3):
                    keep_h0T(at(3))
                if at(1):
                    moments(at(1), 1, x_attended, at(1).count)
                if at(0):
                    leaky(at(0), 0)
                    leaky(at(0), 1)
                if at(1):
                    shift_of(at(1), 1)
                if at(0):
                    row_max(at(0), 0)
                    leaky(at(0), 2)
                    row_max(at(0), 1)

            slots(dve, slot)


def gru_layer(nc, io, t, psum):
    with ExitStack() as ctx:
        def pair(name, shape, dt=F32):
            return [ctx.enter_context(nc.sbuf_tensor(f"{name}{s}", shape, dt)) for s in range(STREAMS)]

        def sem(name):
            return ctx.enter_context(nc.semaphore(name))

        h = pair("h", [128, COLS])
        hp = pair("h_parts", [128, 2, COLS], F16)
        hn = pair("h_nodes", [128, 2, GROUP, DIM], F16)
        tp = pair("t_parts", [128, 2, COLS], F16)
        r = pair("r", [128, COLS])
        z = pair("z", [128, COLS])
        zc = pair("zc", [128, COLS])
        zh = pair("zh", [128, COLS])
        cand = pair("cand", [128, COLS])
        new = pair("new", [128, COLS])
        out = pair("out", [128, GROUP, DIM])

        hi_ready = sem("hi_ready")
        lo_ready = sem("lo_ready")
        turned = sem("turned")
        nodes_ready = sem("nodes_ready")
        t_psum = sem("t_psum")
        t_hi = sem("t_hi")
        t_lo = sem("t_lo")
        r_psum = sem("r_psum")
        z_psum = sem("z_psum_gru")
        n_psum = sem("n_psum")
        r_ready = sem("r_ready")
        z_ready = sem("z_ready_gru")
        zc_ready = sem("zc_ready")
        zh_ready = sem("zh_ready")
        gated = sem("gated")
        summed = sem("summed")
        cand_ready = sem("cand_ready")
        mixed = sem("mixed")
        h_ready = sem("h_ready")
        back_psum = sem("back_psum")
        out_ready = sem("out_ready")
        stored = [sem(f"stored{s}") for s in range(STREAMS)]

        R, Z, N, T = range(BANKS)
        LAST = SLOTS - STREAMS
        gb = t["gates_b"]

        def col(i):
            return gb[:, i:i + 1]

        def at(p, k):
            return (p - 1, k + SLOTS) if k < 0 else (p + 1, k - SLOTS) if k >= SLOTS else (p, k)

        def nth(p, k):
            return p * SLOTS + (k + 1)

        def group_nth(p, s):
            return p * STREAMS + (s + 1)

        def group(p, s):
            return bass.ds(p * (STREAMS * GROUP) + s * GROUP, GROUP)

        def by_graph(x):
            return x.rearrange("p (g n) -> p g n", g=GROUP)

        def h_in(p, k):
            return t["h0T"][:, group(p, k), :] if k < STREAMS else by_graph(h[k % 2][:, :])

        def pairs(eng, pair_of_slots):
            pair_of_slots(0, False, True)
            with eng.Fori(1, PAIRS - 1) as p:
                pair_of_slots(p, True, True)
            pair_of_slots(PAIRS - 1, True, False)

        block = ctx.enter_context(nc.Block())

        @block.tensor
        def _(pe):
            def gate(bank, which, step, parts, terms, start=False, stop=False):
                for n, (w, m) in enumerate(terms):
                    last = mm(nc, bank, t["gru_w"][:, w, step, which * DIM:(which + 1) * DIM], parts[:, m, :],
                              start and n == 0, stop and n == len(terms) - 1)
                return last

            HI, LO = [(0, 0), (1, 0)], [(0, 1)]

            def back(p, s):
                pe.wait_ge(h_ready, nth(p, LAST + s))
                for g in range(GROUP):
                    last = nc.tensor.transpose(psum[:, s, N, g * 128:(g + 1) * 128], h[s][:, g * 128:(g + 1) * 128],
                                               t["ident"][:, :])
                last.then_inc(back_psum, 1)

            def slot(p, k, before):
                s, step = k % 2, k // 2
                bank = [psum[:, s, b, :] for b in range(BANKS)]
                turn = bank[T].bitcast(F16).rearrange("p (m g c) -> p m g c", m=2, g=GROUP)
                if k < STREAMS and before:
                    back(p - 1, s)
                pe.wait_ge(hi_ready, nth(p, k))
                for g in range(GROUP):
                    nc.tensor.transpose(turn[:, 0, g, :], hp[s][:, 0, g * 128:(g + 1) * 128], t["ident16"][:, :])
                gate(bank[R], 0, GRU_STEPS, hp[s], HI, start=True)
                pe.wait_ge(lo_ready, nth(p, k))
                for g in range(GROUP):
                    last = nc.tensor.transpose(turn[:, 1, g, :], hp[s][:, 1, g * 128:(g + 1) * 128], t["ident16"][:, :])
                last.then_inc(turned, 1)
                gate(bank[R], 0, GRU_STEPS, hp[s], LO)
                gate(bank[Z], 1, GRU_STEPS, hp[s], HI + LO, start=True)
                pe.wait_ge(nodes_ready, nth(p, k))
                for g in range(GROUP):
                    for m in range(2):
                        last = mm(nc, bank[T][:, g * 128:(g + 1) * 128], hn[s][:, m, g, :],
                                  t["edges"][:, p * (STREAMS * GROUP) + (s * GROUP + g), :], m == 0, m == 1)
                last.then_inc(t_psum, 1)
                if k < STREAMS and before:
                    pe.wait_ge(out_ready, group_nth(p - 1, s))
                gate(bank[N], 2, GRU_STEPS, hp[s], HI + LO, start=True, stop=True)
                pe.wait_ge(t_hi, nth(p, k))
                gate(bank[R], 0, step, tp[s], HI)
                gate(bank[Z], 1, step, tp[s], HI[:1])
                pe.wait_ge(t_lo, nth(p, k))
                gate(bank[R], 0, step, tp[s], LO, stop=True).then_inc(r_psum, 1)
                gate(bank[Z], 1, step, tp[s], HI[1:] + LO, stop=True).then_inc(z_psum, 1)
                gate(bank[T], 2, step, tp[s], HI + LO, start=True, stop=True).then_inc(n_psum, 1)

            def pair_of_slots(p, before, after):
                for k in range(SLOTS):
                    slot(p, k, before)

            pairs(pe, pair_of_slots)
            for s in range(STREAMS):
                back(PAIRS - 1, s)

        @block.scalar
        def _(act):
            def candidate(p, k):
                act.wait_ge(summed, nth(p, k))
                nc.scalar.activation(cand[k % 2][:, :], new[k % 2][:, :], ACT.Tanh, bias=col(B_IN), scale=col(UNSCALE))\
                    .then_inc(cand_ready, 1)

            def pair_of_slots(p, before, after):
                for k in range(SLOTS):
                    s = k % 2
                    if k or before:
                        candidate(*at(p, k - 1))
                    act.wait_ge(t_psum, nth(p, k))
                    nc.scalar.copy(tp[s][:, 0, :], psum[:, s, T, :]).then_inc(t_hi, 1)
                    act.wait_ge(r_psum, nth(p, k))
                    nc.scalar.activation(r[s][:, :], psum[:, s, R, :], ACT.Sigmoid, bias=col(B_R), scale=col(UNSCALE))\
                        .then_inc(r_ready, 1)
                    act.wait_ge(z_psum, nth(p, k))
                    nc.scalar.activation(z[s][:, :], psum[:, s, Z, :], ACT.Sigmoid, bias=col(B_Z), scale=col(UNSCALE))\
                        .then_inc(z_ready, 1)
                    nc.scalar.activation(zc[s][:, :], psum[:, s, Z, :], ACT.Sigmoid, bias=col(B_NZ),
                                         scale=col(N_UNSCALE)).then_inc(zc_ready, 1)

            act.preload_act_table_set("sigmoid_and_others")
            pairs(act, pair_of_slots)
            candidate(PAIRS - 1, SLOTS - 1)

        @block.gpsimd
        def _(pool):
            with pool.Fori(0, PAIRS) as p:
                for k in range(SLOTS):
                    s = k % 2
                    pool.wait_ge(z_ready, nth(p, k))
                    pool.tensor_tensor(by_graph(zh[s][:, :]), by_graph(z[s][:, :]), h_in(p, k), ALU.mult)\
                        .then_inc(zh_ready, 1)
                    pool.wait_ge(mixed, nth(p, k))
                    pool.wait_ge(zh_ready, nth(p, k))
                    pool.tensor_tensor(h[s][:, :], cand[s][:, :], zh[s][:, :], ALU.add).then_inc(h_ready, 1)

        @block.vector
        def _(dve):
            v = nc.vector

            def split_hi(p, k):
                hi = hp[k % 2][:, 0, :]
                if k < STREAMS:
                    v.tensor_copy(by_graph(hi), h_in(p, k)).then_inc(hi_ready, 1)
                else:
                    dve.wait_ge(mixed, nth(p, k - STREAMS))
                    dve.wait_ge(zh_ready, nth(p, k - STREAMS))
                    v.tensor_tensor(hi, cand[k % 2][:, :], zh[k % 2][:, :], ALU.add).then_inc(hi_ready, 1)

            def split_lo(p, k):
                if k >= STREAMS:
                    dve.wait_ge(h_ready, nth(p, k - STREAMS))
                dve.wait_ge(hi_ready, nth(p, k))
                v.tensor_tensor(by_graph(hp[k % 2][:, 1, :]), h_in(p, k), by_graph(hp[k % 2][:, 0, :]), ALU.subtract)\
                    .then_inc(lo_ready, 1)

            def add_input(p, k):
                s = k % 2
                dve.wait_ge(gated, nth(p, k))
                dve.wait_ge(n_psum, nth(p, k))
                v.tensor_tensor(new[s][:, :], psum[:, s, T, :], r[s][:, :], ALU.add).then_inc(summed, 1)

            def mix(p, k):
                s = k % 2
                dve.wait_ge(cand_ready, nth(p, k))
                dve.wait_ge(zc_ready, nth(p, k))
                v.tensor_tensor(cand[s][:, :], cand[s][:, :], zc[s][:, :], ALU.mult).then_inc(mixed, 1)

            def finish(p, s):
                dve.wait_ge(back_psum, group_nth(p, s))
                dve.wait_ge(stored[s], 16 * p + 16)
                for g in range(GROUP):
                    graph = p * (STREAMS * GROUP) + (s * GROUP + g)
                    last = v.scalar_tensor_tensor(out[s][:, g, :], psum[:, s, N, g * 128:(g + 1) * 128],
                                                  t["mask"][:, bass.ds(graph, 1)], t["x"][:, graph, :],
                                                  ALU.mult, ALU.add)
                last.then_inc(out_ready, 1)

            def pair_of_slots(p, before, after):
                for k in range(SLOTS):
                    s = k % 2
                    tail = k > 0 or before
                    if tail:
                        add_input(*at(p, k - 1))
                    dve.wait_ge(turned, nth(p, k))
                    v.tensor_copy(hn[s][:, :, :, :].rearrange("p m g c -> p (m g c)"), psum[:, s, T, :].bitcast(F16))\
                        .then_inc(nodes_ready, 1)
                    if k < STREAMS and before:
                        finish(p - 1, s)
                    if tail:
                        mix(*at(p, k - 1))
                    dve.wait_ge(t_hi, nth(p, k))
                    v.tensor_tensor(tp[s][:, 1, :], psum[:, s, T, :], tp[s][:, 0, :], ALU.subtract).then_inc(t_lo, 1)
                    if k + 1 < SLOTS or after:
                        split_hi(*at(p, k + 1))
                        split_lo(*at(p, k + 1))
                    dve.wait_ge(r_ready, nth(p, k))
                    v.scalar_tensor_tensor(r[s][:, :], psum[:, s, N, :], col(B_HN), r[s][:, :], ALU.add, ALU.mult)\
                        .then_inc(gated, 1)

            for s in range(STREAMS):
                dve.sem_inc(stored[s], 16)
            split_hi(0, 0)
            split_lo(0, 0)
            pairs(dve, pair_of_slots)
            add_input(PAIRS - 1, SLOTS - 1)
            mix(PAIRS - 1, SLOTS - 1)
            for s in range(STREAMS):
                finish(PAIRS - 1, s)

        @block.sync
        def _(sp):
            with sp.Fori(0, PAIRS) as p:
                for s in range(STREAMS):
                    sp.wait_ge(out_ready, group_nth(p, s))
                    sp.dma_start(io["out"][group(p, s)].rearrange("g n d -> n g d"), out[s][:, :, :])\
                        .then_inc(stored[s], 16)
            for s in range(STREAMS):
                sp.wait_ge(stored[s], 16 * PAIRS + 16)


NAMES = ["x", "adj", "nodemask", "L0_gnn_W", "L0_gnn_a", "L1_gnn_eps", "L1_gnn_W1", "L1_gnn_b1", "L1_gnn_W2",
         "L1_gnn_b2", "L2_gnn_weight", "L2_gnn_bias", "L3_gnn_weight", "L3_gnn_w_ih", "L3_gnn_w_hh", "L3_gnn_b_ih",
         "L3_gnn_b_hh"]


def kernel(**inputs):
    import numpy as np
    import concourse.bacc as bacc
    from concourse.bass_utils import run_bass_kernel_spmd

    nc = bacc.Bacc("TRN2", target_bir_lowering=False, num_devices=1)
    arrays, io = {}, {}
    for name in NAMES:
        a = np.ascontiguousarray(inputs[name])
        arrays[f"in_{name}"] = a
        io[name] = nc.dram_tensor(f"in_{name}", a.shape, mybir.dt.from_np(a.dtype), kind="ExternalInput").ap()
    io["out"] = nc.dram_tensor("out_x", (GRAPHS, NODES, DIM), F32, kind="ExternalOutput").ap()
    build(nc, io)
    got = run_bass_kernel_spmd(nc, [arrays], core_ids=[0])
    return got.results[0]["out_x"]
```

```python
from contextlib import ExitStack

import concourse.bass as bass
from concourse import mybir
from concourse.alu_op_type import AluOpType as ALU

ACT = mybir.ActivationFunctionType
AXIS = mybir.AxisListType
F32 = mybir.dt.float32
F16 = mybir.dt.float16
BF16 = mybir.dt.bfloat16
I32 = mybir.dt.int32

GRAPHS, NODES, DIM = 64, 128, 128
HEADS = 4
HEAD_DIM = DIM // HEADS
HIDDEN = 256
GRU_STEPS = 5
GATES = 3
GROUP = 4
GROUPS = GRAPHS // GROUP
COLS = GROUP * NODES
STREAMS = 4
ROUNDS = GROUPS // STREAMS
BANKS = 4
SLOTS = STREAMS * GRU_STEPS
LOOP_FROM = 2
EPS = 1e-5
SLOPE = 0.2
MASKED = -(2.0 ** 120)
LO_ROW = 32
SCALE_EXP = 12
SCORE_EXP = 7
LEAST = 2.0 ** -60


def mm(nc, out, lhsT, rhs, start=True, stop=True):
    return nc.tensor.matmul(out, lhsT, rhs, start=start, stop=stop)


def build(nc, io):
    with ExitStack() as ctx:
        def sb(name, shape, dt=F32):
            return ctx.enter_context(nc.sbuf_tensor(name, shape, dt))

        t = {}
        t["x"] = sb("x_all", [128, GRAPHS, DIM])
        t["edges"] = sb("edges", [128, GRAPHS, NODES], F16)
        t["h0T"] = sb("h0T", [128, GRAPHS, NODES])
        t["ident"] = sb("ident", [128, 128])
        t["ident16"] = sb("ident16", [128, 128], F16)
        t["identb"] = sb("identb", [128, 128], BF16)
        t["W0"] = sb("W0", [128, DIM])
        t["score_w"] = sb("score_w", [128, 128])
        t["pick_i"] = sb("pick_i", [128, HEADS, 128], F16)
        t["pick_j"] = sb("pick_j", [128, HEADS, 128], F16)
        t["self_eye"] = sb("self_eye", [128, 128])
        t["W1"] = sb("W1", [128, HIDDEN])
        t["W2"] = sb("W2", [128, 2, DIM])
        t["b1"] = sb("b1", [128, 2])
        t["b2"] = sb("b2", [128, DIM])
        t["W3"] = sb("W3", [128, DIM])
        t["b3"] = sb("b3", [128, DIM])
        t["gru_w"] = sb("gru_w", [128, 2, GRU_STEPS + 1, GATES * DIM], F16)
        t["gates_b"] = sb("gates_b", [128, 9])
        t["mask"] = sb("mask", [128, GRAPHS])
        psum = ctx.enter_context(nc.psum_tensor("psum", [128, 2, BANKS, 512], F32))
        with ExitStack() as until_gru:
            gru = GruWeights(nc, io, t, psum, until_gru)
            prologue(nc, io, t, psum, gru)
            first_layers(nc, io, t, psum, gru)
        gru_layer(nc, io, t, psum)


B_R, B_Z, B_NZ, B_IN, B_HN, UNSCALE, N_UNSCALE, SCALE, E_UNSCALE = range(9)


def chain(eng, link):
    done = [0]

    def linked(ins):
        done[0] += 1
        ins.then_inc(link, 1)
        eng.wait_ge(link, done[0])
    return linked


def power_of_two(v, linked, largest, bits, exp, scale, unscale):
    linked(v.tensor_copy(bits[:, 0:1], largest.bitcast(I32)))
    linked(v.tensor_scalar(bits[:, 1:2], bits[:, 0:1], 0x7F800000, None, ALU.bitwise_and))
    linked(v.tensor_scalar(bits[:, 2:3], bits[:, 1:2], -1.0, float((254 + exp) << 23), ALU.mult, ALU.add))
    linked(v.tensor_scalar(bits[:, 3:4], bits[:, 1:2], float(-(exp << 23)), None, ALU.add))
    linked(v.tensor_copy(scale, bits[:, 2:3].bitcast(F32)))
    linked(v.tensor_copy(unscale, bits[:, 3:4].bitcast(F32)))


class GruWeights:

    def __init__(self, nc, io, t, psum, ctx):
        def sb(name, shape, dt=F32):
            return ctx.enter_context(nc.sbuf_tensor(name, shape, dt))

        def sem(name):
            return ctx.enter_context(nc.semaphore(name))

        self.nc, self.t = nc, t
        self.P = psum[:, :, :, :].rearrange("p s b c -> p (s b) c")
        self.gw = sb("gw", [128, GRU_STEPS, DIM])
        self.wi = sb("wi", [128, GATES, DIM])
        self.wh = sb("wh", [128, GATES, DIM])
        self.gwT = sb("gwT", [128, GRU_STEPS, DIM])
        self.wiT = sb("wiT", [128, GATES * DIM])
        self.bi = sb("bi", [128, GATES])
        self.bh = sb("bh", [128, GATES])
        self.nm = sb("nm", [64, 128])
        self.gf = sb("gf", [128, GRU_STEPS + 1, GATES * DIM])
        self.tops = sb("tops", [128, GRU_STEPS + 1])
        self.top = sb("top", [128, 1])
        self.top1 = sb("top1", [1, 2])
        self.bits = sb("bits", [128, 4], I32)
        self.ones = sb("ones", [1, 128])
        self.loaded = sem("later_weights_loaded")
        self.turned = sem("weights_transposed")
        self.kept = sem("transposes_kept")
        self.fused = sem("gru_weights_fused")
        self.fused_kept = sem("gru_weights_kept")
        self.maxed = sem("row_max_kept_gru")
        self.scale_step = sem("scale_pe_gru")
        self.link = sem("vector_link_gru")
        self.scaled = sem("gru_weights_scaled")
        self.loads = [
            (self.gw[:, :, :], io["L3_gnn_weight"].rearrange("l d e -> d l e")),
            (self.wi[:, :, :], io["L3_gnn_w_ih"].rearrange("(t c) e -> c t e", t=GATES)),
            (self.wh[:, :, :], io["L3_gnn_w_hh"].rearrange("(t c) e -> c t e", t=GATES)),
            (t["W1"][:, :], io["L1_gnn_W1"][:, :]),
            (t["W2"][:, :, :], io["L1_gnn_W2"].rearrange("(t k) d -> k t d", t=2)),
            (t["b2"][:, :], io["L1_gnn_b2"][:].partition_broadcast(128)),
            (t["W3"][:, :], io["L2_gnn_weight"][:, :]),
            (t["b3"][:, :], io["L2_gnn_bias"][:].partition_broadcast(128)),
            (self.nm[:, :], io["nodemask"][:, :]),
        ]
        self.columns = [
            (t["b1"][:, :], io["L1_gnn_b1"].rearrange("(t p) -> p t", t=2)),
            (self.bi[:, :], io["L3_gnn_b_ih"].rearrange("(t p) -> p t", t=GATES)),
            (self.bh[:, :], io["L3_gnn_b_hh"].rearrange("(t p) -> p t", t=GATES)),
        ]
        self.all_loaded = 16 * (len(self.loads) + len(self.columns))
        self.fused_banks = [0, 1, 2, 3, 6]
        self.small_bank = 6

    def turn(self, pe):
        P, ident = self.P, self.t["ident"]
        pe.wait_ge(self.loaded, self.all_loaded)
        sources = [self.gw[:, l, :] for l in range(GRU_STEPS)] + [self.wi[:, k, :] for k in range(GATES)] + \
                  [self.wh[:, k, :] for k in range(GATES)]
        for k, src in enumerate(sources):
            self.nc.tensor.transpose(P[:, k // 4, k % 4 * 128:(k % 4 + 1) * 128], src, ident[:, :])
        self.nc.tensor.transpose(P[:, 2, 384:384 + GRAPHS], self.nm[:, :], ident[0:64, 0:64]).then_inc(self.turned, 1)

    def keep(self, dve):
        v, P = self.nc.vector, self.P
        dve.wait_ge(self.turned, 1)
        v.tensor_copy(self.gwT[:, 0:4, :], P[:, 0, :].rearrange("p (l e) -> p l e", l=4))
        v.tensor_copy(self.gwT[:, 4, :], P[:, 1, 0:128])
        v.tensor_copy(self.wiT[:, :], P[:, 1, 128:512])
        v.tensor_copy(self.gf[:, GRU_STEPS, :], P[:, 2, 0:384])
        v.tensor_copy(self.t["mask"][:, :], P[:, 2, 384:384 + GRAPHS]).then_inc(self.kept, 1)

    def fuse(self, pe):
        pe.wait_ge(self.kept, 1)
        for l, bank in enumerate(self.fused_banks):
            mm(self.nc, self.P[:, bank, 0:GATES * DIM], self.gwT[:, l, :], self.wiT[:, :]).then_inc(self.fused, 1)

    def keep_fused(self, dve):
        v = self.nc.vector
        for l, bank in enumerate(self.fused_banks):
            dve.wait_ge(self.fused, l + 1)
            v.tensor_copy(self.gf[:, l, :], self.P[:, bank, 0:GATES * DIM]).then_inc(self.fused_kept, 1)
            v.tensor_reduce(self.tops[:, l:l + 1], self.P[:, bank, 0:GATES * DIM], AXIS.X, ALU.max,
                            apply_absolute_value=True)
        v.tensor_reduce(self.tops[:, GRU_STEPS:], self.gf[:, GRU_STEPS, :], AXIS.X, ALU.max,
                        apply_absolute_value=True).then_inc(self.maxed, 1)
        dve.wait_ge(self.maxed, 1)
        v.tensor_reduce(self.top[:, 0:1], self.tops[:, :], AXIS.X, ALU.max).then_inc(self.maxed, 1)

    def turn_max(self, pe):
        pe.wait_ge(self.maxed, 2)
        self.nc.tensor.transpose(self.P[0:1, self.small_bank, 0:128], self.top[:, 0:1], self.t["ident"][:, :])\
            .then_inc(self.scale_step, 1)

    def whole_max(self, dve):
        v = self.nc.vector
        dve.wait_ge(self.scale_step, 1)
        v.tensor_reduce(self.top1[:, 1:2], self.P[0:1, self.small_bank, 0:128], AXIS.X, ALU.max).then_inc(self.maxed, 1)
        dve.wait_ge(self.maxed, 3)
        v.tensor_scalar(self.top1[:, 0:1], self.top1[:, 1:2], LEAST, None, ALU.max).then_inc(self.maxed, 1)

    def spread_max(self, pe):
        pe.wait_ge(self.maxed, 4)
        mm(self.nc, self.P[:, self.small_bank, 256:257], self.ones[:, :], self.top1[:, 0:1])\
            .then_inc(self.scale_step, 1)

    def scale(self, dve):
        v, gb, bi, bh = self.nc.vector, self.t["gates_b"], self.bi, self.bh
        scale = gb[:, SCALE:SCALE + 1]
        linked = chain(dve, self.link)
        linked(v.tensor_tensor(gb[:, B_R:B_Z + 1], bi[:, 0:2], bh[:, 0:2], ALU.add))
        linked(v.tensor_scalar(gb[:, B_NZ:B_NZ + 1], gb[:, B_Z:B_Z + 1], -1.0, None, ALU.mult))
        linked(v.tensor_copy(gb[:, B_IN:B_IN + 1], bi[:, 2:3]))
        dve.wait_ge(self.scale_step, 2)
        power_of_two(v, linked, self.P[:, self.small_bank, 256:257], self.bits, SCALE_EXP, scale,
                     gb[:, UNSCALE:UNSCALE + 1])
        linked(v.tensor_scalar(gb[:, N_UNSCALE:N_UNSCALE + 1], gb[:, UNSCALE:UNSCALE + 1], -1.0, None, ALU.mult))
        linked(v.tensor_scalar(gb[:, B_HN:B_HN + 1], bh[:, 2:3], scale, None, ALU.mult))
        dve.sem_inc(self.scaled, 1)

    def split(self, dve):
        v, gf, gru_w = self.nc.vector, self.gf, self.t["gru_w"]
        scale = self.t["gates_b"][:, SCALE:SCALE + 1]
        v.tensor_scalar(gru_w[:, 0, :, :], gf[:, :, :], scale, None, ALU.mult).then_inc(self.scaled, 1)
        dve.wait_ge(self.scaled, 2)
        v.scalar_tensor_tensor(gru_w[:, 1, :, :], gf[:, :, :], scale, gru_w[:, 0, :, :], ALU.mult, ALU.subtract)


def prologue(nc, io, t, psum, gru):
    with ExitStack() as ctx:
        def sb(name, shape, dt=F32):
            return ctx.enter_context(nc.sbuf_tensor(name, shape, dt))

        def sem(name):
            return ctx.enter_context(nc.semaphore(name))

        a1 = sb("a1", [128, DIM])
        a2 = sb("a2", [128, DIM])
        wa = sb("wa", [128, 2, DIM])
        was = sb("was", [128, 2, HEADS])
        eps = sb("eps", [128, 1])
        top = sb("top_score", [128, 1])
        top1 = sb("top1_score", [1, 2])
        bits = sb("bits_score", [128, 4], I32)
        ones = gru.ones
        loaded = sem("weights_loaded")
        made = sem("constants_made")
        maxed = sem("row_max_kept")
        scale_step = sem("scale_pe")
        link = sem("vector_link")
        glink = sem("gpsimd_link")
        P = psum[:, :, :, :].rearrange("p s b c -> p (s b) c")

        loads = [
            (t["W0"][:, :], io["L0_gnn_W"][:, :]),
            (a1[:, :].rearrange("p (h d) -> p h d", h=HEADS), io["L0_gnn_a"][:, 0:HEAD_DIM].partition_broadcast(128)),
            (a2[:, :].rearrange("p (h d) -> p h d", h=HEADS),
             io["L0_gnn_a"][:, HEAD_DIM:2 * HEAD_DIM].partition_broadcast(128)),
            (eps[:, :], io["L1_gnn_eps"][:].partition_broadcast(128)),
        ]
        block = ctx.enter_context(nc.Block())

        @block.sync
        def _(sp):
            for out, in_ in loads:
                sp.dma_start(out, in_).then_inc(loaded, 16)
            for out, in_ in gru.loads:
                sp.dma_start(out, in_).then_inc(gru.loaded, 16)
            with nc.allow_non_contiguous_dma(reason="bias vectors of 256 or 384 numbers, one per partition"):
                for out, in_ in gru.columns:
                    sp.dma_start(out, in_).then_inc(gru.loaded, 16)

        @block.gpsimd
        def _(pool):
            pool.memset(ones[:, :], 1.0).then_inc(made, 1)
            for k, eye in enumerate((t["ident"], t["ident16"], t["identb"])):
                pool.memset(eye[:, :], 0.0).then_inc(glink, 1)
                pool.wait_ge(glink, k + 1)
                pool.affine_select(out=eye[:, :], in_=eye[:, :], compare_op=ALU.not_equal, fill=1.0, base=0,
                                   pattern=[[-1, 128]], channel_multiplier=1).then_inc(made, 1)
            links = 3
            for pick, row in ((t["pick_i"], 0), (t["pick_j"], HEADS)):
                pool.memset(pick[:, :, :], 0.0).then_inc(glink, 1)
                links += 1
                for part in (0, LO_ROW):
                    pool.wait_ge(glink, links)
                    pool.affine_select(out=pick[:, :, :], in_=pick[:, :, :], compare_op=ALU.not_equal, fill=1.0,
                                       base=-(row + part), pattern=[[-1, HEADS], [0, 128]],
                                       channel_multiplier=1).then_inc(glink, 1)
                    links += 1

        @block.tensor
        def _(pe):
            pe.wait_ge(made, 2)
            pe.wait_ge(maxed, 1)
            nc.tensor.transpose(P[0:1, 0, 0:128], top[:, 0:1], t["ident"][:, :]).then_inc(scale_step, 1)
            pe.wait_ge(maxed, 2)
            mm(nc, P[:, 1, 0:1], ones[:, :], top1[:, 0:1]).then_inc(scale_step, 1)

        @block.vector
        def _(dve):
            linked = chain(dve, link)
            v = nc.vector
            v.memset(t["score_w"][:, :], 0.0)
            dve.wait_ge(loaded, 16 * len(loads))
            linked(v.tensor_tensor(wa[:, 0, :], t["W0"][:, :], a1[:, :], ALU.mult))
            linked(v.tensor_tensor(wa[:, 1, :], t["W0"][:, :], a2[:, :], ALU.mult))
            linked(v.tensor_reduce(was[:, :, :], wa[:, :, :].rearrange("p k (h d) -> p k h d", h=HEADS),
                                   AXIS.X, ALU.add))
            v.tensor_reduce(top[:, 0:1], was[:, :, :].rearrange("p k h -> p (k h)"), AXIS.X, ALU.max,
                            apply_absolute_value=True).then_inc(maxed, 1)
            linked(v.tensor_scalar(eps[:, :], eps[:, :], 1.0, None, ALU.add))
            dve.wait_ge(made, 2)
            linked(v.tensor_scalar(t["self_eye"][:, :], t["ident"][:, :], eps[:, 0:1], None, ALU.mult))
            dve.wait_ge(scale_step, 1)
            linked(v.tensor_reduce(top1[:, 1:2], P[0:1, 0, 0:128], AXIS.X, ALU.max))
            v.tensor_scalar(top1[:, 0:1], top1[:, 1:2], LEAST, None, ALU.max).then_inc(maxed, 1)
            dve.wait_ge(scale_step, 2)
            power_of_two(v, linked, P[:, 1, 0:1], bits, SCORE_EXP, top[:, 0:1],
                         t["gates_b"][:, E_UNSCALE:E_UNSCALE + 1])
            for row in (0, LO_ROW):
                linked(v.tensor_scalar(t["score_w"][:, row:row + 2 * HEADS], was[:, :, :].rearrange("p k h -> p (k h)"),
                                       top[:, 0:1], None, ALU.mult))


def first_layers(nc, io, t, psum, gru):
    with ExitStack() as ctx:
        def one(name, shape, dt=F32):
            return ctx.enter_context(nc.sbuf_tensor(name, shape, dt))

        def two(name, shape, dt=F32):
            return [one(f"{name}{s}", shape, dt) for s in range(2)]

        def sem(name):
            return ctx.enter_context(nc.semaphore(name))

        LAYERS = range(4)
        stats = [one(f"stats{n}", [128, GROUP, 6]) for n in LAYERS]
        mean_var = [one(f"mean_var{n}", [128, GROUP, 2]) for n in LAYERS]
        log_var = [one(f"log_var{n}", [128, GROUP]) for n in LAYERS]
        rstd = [one(f"rstd{n}", [128, GROUP]) for n in LAYERS]
        shift = {n: one(f"shift{n}", [128, GROUP]) for n in (1, 2)}
        y = [one(f"y{n}", [128, GROUP, DIM]) for n in LAYERS]
        hT = one("hT", [128, COLS])
        e_parts = two("e_parts", [128, COLS], F16)
        hW = two("hW", [128, GROUP, HEADS, HEAD_DIM + 1])
        adj = two("adj", [128, GROUP, NODES])
        adjT = two("adjT", [128, GROUP, NODES])
        adjT1 = two("adjT1", [128, GROUP, NODES])
        gone = two("gone", [128, GROUP, NODES], BF16)
        prob = one("prob", [128, GROUP, HEADS, NODES])
        probT = one("probT", [128, GROUP, HEADS, NODES])
        top = one("row_max", [128, GROUP, HEADS])
        rsum = one("rsum", [128, GROUP, HEADS])
        att = one("att", [128, GROUP, HEADS, HEAD_DIM])
        zT = [one(f"zT{n}", [128, GROUP, NODES]) for n in range(2)]
        hid = one("hid", [128, 2, COLS])
        eps_col = one("eps_col", [128, 1])

        x_loaded = [sem(f"x_loaded{s}") for s in range(2)]
        adj_loaded = [sem(f"adj_loaded{s}") for s in range(2)]
        constants = sem("constants")
        passed = {e: sem(f"{e}_passed") for e in ("vector", "scalar", "gpsimd")}
        stats_done = [sem(f"stats_done{n}") for n in LAYERS]
        var_ready = [sem(f"var_ready{n}") for n in LAYERS]
        log_done = [sem(f"log_done{n}") for n in LAYERS]
        rstd_ready = [sem(f"rstd_ready{n}") for n in LAYERS]
        shift_ready = {n: sem(f"shift_ready{n}") for n in (1, 2)}
        y_ready = [sem(f"y_ready{n}") for n in LAYERS]
        centred = {n: sem(f"centred{n}") for n in (0, 3)}
        gone_ready = sem("gone_ready")
        edges_ready = sem("edges_ready")
        yT_psum = sem("yT_psum")
        hT_ready = sem("hT_ready")
        e_psum = sem("e_psum")
        e_hi = sem("e_hi")
        e_lo = sem("e_lo")
        hW_psum = sem("hW_psum")
        hW_ready = sem("hW_ready")
        adjT_psum = sem("adjT_psum")
        adjT_ready = sem("adjT_ready")
        adjT1_ready = sem("adjT1_ready")
        score_ready = sem("score_ready")
        sloped = sem("sloped")
        lrelu_done = sem("lrelu_done")
        max_done = sem("max_done")
        shifted = sem("shifted")
        exp_done = sem("exp_done")
        probT_psum = sem("probT_psum")
        probT_act = sem("probT_act")
        probT_dve = sem("probT_dve")
        att_psum = sem("att_psum")
        rsum_done = sem("rsum_done")
        att_done = sem("att_done")
        x_attended = sem("x_attended")
        biased = [sem(f"biased{n}") for n in range(2)]
        z_psum = [sem(f"z_psum{n}") for n in range(2)]
        z_ready = [sem(f"z_ready{n}") for n in range(2)]
        out_psum = [sem(f"out_psum{n}") for n in range(2)]
        x_added = [sem(f"x_added{n}") for n in range(2)]
        hid_psum = [sem(f"hid_psum{k}") for k in range(2)]
        hid_ready = [sem(f"hid_ready{k}") for k in range(2)]
        h0T_psum = sem("h0T_psum")
        h0T_kept = sem("h0T_kept")

        B_EDGE, B_TURN, B_SUM, B_HW = 4, 5, 6, 7
        P = psum[:, :, :, :].rearrange("p s b c -> p (s b) c")
        BACKS = 4

        class Group:

            def __init__(self, p, q, back):
                self.p, self.q, self.back = p, q, back
                self.number = p * 2 + (q - back)
                self.odd = (q - back) % 2
                self.count = p * 2 + (q - back + 1)
                self.loads = p * 16 + 16 * ((q - back) // 2 + 1)
                self.exists = not isinstance(p, int) or 0 <= self.number < GROUPS
                self.all = bass.ds(self.number * GROUP, GROUP)

            def graph(self, g):
                return self.number * GROUP + g

            def graph_count(self, g):
                return self.number * GROUP + (g + 1)

            def half_count(self, g):
                return self.number * 2 + (g // 2 + 1)

            def before(self, n):
                return Group(self.p, self.q, self.back + n)

        def xs(group):
            return t["x"][:, group.all, :]

        def flat(x):
            return x.rearrange("p g n -> p (g n)")

        def slots(eng, slot):
            def one_slot(p, q, number=None):
                def at(back):
                    group = Group(p, q, back)
                    return group if group.exists else None
                slot(at, number)

            for p in range(LOOP_FROM):
                for q in range(2):
                    one_slot(p, q, p * 2 + q)
            with eng.Fori(LOOP_FROM, GROUPS // 2) as p:
                for q in range(2):
                    one_slot(p, q)
            for q in range(BACKS - 1):
                one_slot(GROUPS // 2, q)

        def wait_users(eng, *users):
            for signal, group in users:
                if group.exists:
                    eng.wait_ge(signal, group.count)
                    return

        def apart(eng, name):
            def wait_apart(signal, count):
                eng.wait_ge(signal, count)
                eng.sem_inc(passed[name], 1)
            return wait_apart

        block = ctx.enter_context(nc.Block())

        @block.sync
        def _(sp):
            def load(p, first):
                for q in range(2):
                    group = Group(p, q, 0)
                    if not first:
                        sp.wait_ge(x_loaded[q], 16 * p)
                    sp.dma_start(xs(group), io["x"][group.all].rearrange("g n d -> n g d")).then_inc(x_loaded[q], 16)
                    if not first:
                        sp.wait_ge(adjT_psum, group.before(2).count)
                        sp.wait_ge(gone_ready, group.before(2).count)
                        sp.wait_ge(edges_ready, group.before(2).count)
                    sp.dma_start(adj[q][:, :, :], io["adj"][group.all].rearrange("g n m -> n g m"))\
                        .then_inc(adj_loaded[q], 16)

            load(0, True)
            with sp.Fori(1, GROUPS // 2) as p:
                load(p, False)

        @block.gpsimd
        def _(pool):
            wait_apart = apart(pool, "gpsimd")

            def add_self(group):
                pool.wait_ge(adjT_ready, group.count)
                if group.before(2).exists:
                    pool.wait_ge(z_psum[0], group.before(2).count)
                pool.tensor_tensor(adjT1[group.odd][:, :, :], adjT[group.odd][:, :, :],
                                   t["self_eye"][:, :].unsqueeze(1).to_broadcast([128, GROUP, 128]), ALU.add)\
                    .then_inc(adjT1_ready, 1)

            def bias(group, n, b):
                wait_apart(y_ready[n + 1], group.count)
                pool.tensor_tensor(xs(group), xs(group), b[:, :].unsqueeze(1).to_broadcast([128, GROUP, DIM]), ALU.add)\
                    .then_inc(biased[n], 1)

            def less_max(group, g):
                pool.wait_ge(max_done, group.graph_count(g))
                pool.tensor_tensor(prob[:, g, :, :], prob[:, g, :, :],
                                   top[:, g, :].unsqueeze(2).to_broadcast([128, HEADS, NODES]),
                                   ALU.subtract).then_inc(shifted, 1)

            def normalise(group, n):
                wait_apart(var_ready[n], group.count)
                if n == 0 and group.before(1).exists:
                    wait_apart(yT_psum, group.before(1).count)
                pool.tensor_tensor(y[n][:, :, :], xs(group), mean_var[n][:, :, 0:1].to_broadcast([128, GROUP, DIM]),
                                   ALU.subtract).then_inc(centred[n], 1)
                pool.wait_ge(rstd_ready[n], group.count)
                pool.wait_ge(centred[n], group.count)
                pool.tensor_tensor(y[n][:, :, :], y[n][:, :, :],
                                   rstd[n][:, :].unsqueeze(2).to_broadcast([128, GROUP, DIM]), ALU.mult)\
                    .then_inc(y_ready[n], 1)

            def slot(at, number):
                if at(2):
                    add_self(at(2))
                if at(3):
                    bias(at(3), 1, t["b3"])
                if at(0):
                    normalise(at(0), 0)
                if at(1):
                    less_max(at(1), 0)
                    less_max(at(1), 1)
                if at(2):
                    bias(at(2), 0, t["b2"])
                if at(1):
                    less_max(at(1), 2)
                    less_max(at(1), 3)
                if at(3):
                    normalise(at(3), 3)

            pool.memset(eps_col[:, :], EPS).then_inc(constants, 1)
            for s in range(2):
                pool.memset(hW[s][:, :, :, HEAD_DIM:], 1.0).then_inc(constants, 1)
            pool.wait_ge(constants, 3)
            pool.wait_ge(gru.loaded, gru.all_loaded)
            slots(pool, slot)

        @block.tensor
        def _(pe):
            def turn(bank, src):
                for g in range(GROUP):
                    last = nc.tensor.transpose(P[:, bank, g * 128:(g + 1) * 128], src[:, g, :], t["ident"][:, :])
                return last

            def turn_y0(group):
                pe.wait_ge(y_ready[0], group.count)
                wait_users(pe, (h0T_kept, group.before(4)), (x_added[0], group.before(3)), (hT_ready, group.before(1)))
                turn(B_TURN, y[0]).then_inc(yT_psum, 1)

            def score_terms(group):
                pe.wait_ge(hT_ready, group.count)
                wait_users(pe, (x_added[1], group.before(3)), (e_lo, group.before(1)))
                mm(nc, P[:, B_EDGE, :], t["score_w"][:, :], hT[:, :]).then_inc(e_psum, 1)

            def project(group):
                pe.wait_ge(hT_ready, group.count)
                wait_users(pe, (adjT_ready, group.before(1)))
                for g in range(GROUP):
                    last = mm(nc, P[:, B_HW, g * 128:(g + 1) * 128], hT[:, g * 128:(g + 1) * 128], t["W0"][:, :])
                last.then_inc(hW_psum, 1)

            def turn_adj(group):
                pe.wait_ge(adj_loaded[group.odd], group.loads)
                wait_users(pe, (hW_ready, group))
                turn(B_HW, adj[group.odd]).then_inc(adjT_psum, 1)

            def scores(group, g):
                pe.wait_ge(gone_ready, group.count)
                pe.wait_ge(e_hi, group.count)
                pe.wait_ge(e_lo, group.count)
                wait_users(pe, (att_done, group.before(1)))
                bank = P[:, g, :].rearrange("p (h m) -> p h m", h=HEADS)
                e = e_parts[group.odd][:, g * 128:(g + 1) * 128]
                mm(nc, bank, t["identb"][:, :],
                   gone[group.odd][:, g, :].unsqueeze(1).to_broadcast([128, HEADS, NODES]), True, False)
                mm(nc, bank, e, t["pick_i"][:, :, :], False, False)
                for h in range(HEADS):
                    last = mm(nc, bank[:, h, :], t["pick_j"][:, h, :], e, False, h == HEADS - 1)
                last.then_inc(score_ready, 1)

            def turn_prob(group, g):
                pe.wait_ge(exp_done, group.graph_count(g))
                for h in range(HEADS):
                    last = nc.tensor.transpose(P[:, g, h * 128:(h + 1) * 128], prob[:, g, h, :], t["ident"][:, :])
                last.then_inc(probT_psum, 1)

            def attend(group, g):
                pe.wait_ge(probT_dve if g % 2 else probT_act, group.half_count(g))
                pe.wait_ge(hW_ready, group.count)
                for h in range(HEADS):
                    last = mm(nc, P[:, g, h * (HEAD_DIM + 1):(h + 1) * (HEAD_DIM + 1)], probT[:, g, h, :],
                              hW[group.odd][:, g, h, :])
                if g == GROUP - 1:
                    last.then_inc(att_psum, 1)

            def neighbours(group, n, bank, near, signal):
                pe.wait_ge(y_ready[n + 1], group.count)
                pe.wait_ge(signal, group.count)
                if n == 1:
                    wait_users(pe, (e_lo, group.before(-2)), (x_added[1], group.before(1)))
                else:
                    wait_users(pe, (hid_ready[1], group.before(1)))
                for g in range(GROUP):
                    last = mm(nc, P[:, bank, g * 128:(g + 1) * 128], y[n + 1][:, g, :], near[:, g, :])
                last.then_inc(z_psum[n], 1)

            def hidden(group, k, bank):
                pe.wait_ge(z_ready[0], group.count)
                if k == 0:
                    wait_users(pe, (hT_ready, group.before(-2)), (h0T_kept, group.before(2)))
                mm(nc, P[:, bank, :], t["W1"][:, k * 128:(k + 1) * 128], flat(zT[0][:, :, :]))\
                    .then_inc(hid_psum[k], 1)

            def out_0(group):
                pe.wait_ge(hid_ready[0], group.count)
                pe.wait_ge(hid_ready[1], group.count)
                for g in range(GROUP):
                    for k in range(2):
                        last = mm(nc, P[:, B_TURN, g * 128:(g + 1) * 128], hid[:, k, g * 128:(g + 1) * 128],
                                  t["W2"][:, k, :], k == 0, k == 1)
                last.then_inc(out_psum[0], 1)

            def out_1(group):
                pe.wait_ge(z_ready[1], group.count)
                for g in range(GROUP):
                    last = mm(nc, P[:, B_EDGE, g * 128:(g + 1) * 128], zT[1][:, g, :], t["W3"][:, :])
                last.then_inc(out_psum[1], 1)

            def turn_y3(group):
                pe.wait_ge(y_ready[3], group.count)
                wait_users(pe, (x_added[0], group.before(-1)), (h0T_kept, group.before(1)))
                turn(B_TURN, y[3]).then_inc(h0T_psum, 1)

            def slot(at, number):
                if number == 0:
                    gru.turn(pe)
                    gru.fuse(pe)
                if number == 2:
                    pe.wait_ge(gru.scaled, 1)
                if at(1):
                    project(at(1))
                if at(3):
                    neighbours(at(3), 1, B_EDGE, adjT[at(3).odd], adjT_ready)
                if at(1):
                    scores(at(1), 0)
                    scores(at(1), 1)
                if at(3):
                    out_1(at(3))
                if at(1):
                    scores(at(1), 2)
                    scores(at(1), 3)
                    turn_adj(at(1))
                if at(0):
                    turn_y0(at(0))
                if at(2):
                    neighbours(at(2), 0, B_SUM, adjT1[at(2).odd], adjT1_ready)
                if at(0):
                    score_terms(at(0))
                if number == 0:
                    gru.turn_max(pe)
                    gru.spread_max(pe)
                if at(2):
                    hidden(at(2), 1, B_SUM)
                    hidden(at(2), 0, B_TURN)
                if at(1):
                    turn_prob(at(1), 0)
                    turn_prob(at(1), 1)
                if at(2):
                    out_0(at(2))
                if at(1):
                    attend(at(1), 0)
                    turn_prob(at(1), 2)
                    turn_prob(at(1), 3)
                    attend(at(1), 1)
                    attend(at(1), 2)
                    attend(at(1), 3)
                if at(3):
                    turn_y3(at(3))

            pe.wait_ge(constants, 3)
            slots(pe, slot)

        @block.scalar
        def _(act):
            a = nc.scalar
            wait_apart = apart(act, "scalar")

            def rstd_of(group, n):
                act.wait_ge(var_ready[n], group.count)
                a.activation(log_var[n][:, :], mean_var[n][:, :, 1], ACT.Ln, bias=eps_col[:, 0:1])\
                    .then_inc(log_done[n], 1)
                act.wait_ge(log_done[n], group.count)
                a.activation(rstd[n][:, :], log_var[n][:, :], ACT.Exp, scale=-0.5).then_inc(rstd_ready[n], 1)

            def normalise(group, n):
                wait_apart(shift_ready[n], group.count)
                for g in range(GROUP):
                    last = a.activation(y[n][:, g, :], t["x"][:, group.graph(g), :], ACT.Relu,
                                        bias=shift[n][:, g:g + 1], scale=rstd[n][:, g:g + 1])
                last.then_inc(y_ready[n], 1)

            def keep_hT(group):
                act.wait_ge(yT_psum, group.count)
                if group.before(1).exists:
                    act.wait_ge(e_psum, group.before(1).count)
                    act.wait_ge(hW_psum, group.before(1).count)
                a.activation(hT[:, :], P[:, B_TURN, :], ACT.Relu).then_inc(hT_ready, 1)

            def keep_e(group):
                act.wait_ge(e_psum, group.count)
                if group.before(2).exists:
                    act.wait_ge(score_ready, group.before(2).graph_count(GROUP - 1))
                a.copy(e_parts[group.odd][:, :], P[:, B_EDGE, :]).then_inc(e_hi, 1)

            def keep_hW(group):
                act.wait_ge(hW_psum, group.count)
                if group.before(2).exists:
                    act.wait_ge(att_psum, group.before(2).count)
                a.copy(hW[group.odd][:, :, :, 0:HEAD_DIM],
                       P[:, B_HW, :].rearrange("p (g h d) -> p g h d", g=GROUP, h=HEADS)).then_inc(hW_ready, 1)

            def keep_adjT(group):
                act.wait_ge(adjT_psum, group.count)
                if group.before(2).exists:
                    act.wait_ge(z_psum[1], group.before(2).count)
                a.copy(flat(adjT[group.odd][:, :, :]), P[:, B_HW, :]).then_inc(adjT_ready, 1)

            def slope(group, g):
                act.wait_ge(score_ready, group.graph_count(g))
                a.activation(prob[:, g, :, :].rearrange("p h m -> p (h m)"), P[:, g, :], ACT.Copy, scale=SLOPE)\
                    .then_inc(sloped, 1)

            def exponential(group, g):
                act.wait_ge(shifted, group.graph_count(g))
                a.activation(prob[:, g, :, :], prob[:, g, :, :], ACT.Exp, scale=t["gates_b"][:, E_UNSCALE:E_UNSCALE + 1])\
                    .then_inc(exp_done, 1)

            def keep_probT(group, g):
                act.wait_ge(probT_psum, group.graph_count(g))
                a.copy(probT[:, g, :, :].rearrange("p h n -> p (h n)"), P[:, g, :]).then_inc(probT_act, 1)

            def keep_z(group, n, bank):
                act.wait_ge(z_psum[n], group.count)
                a.copy(flat(zT[n][:, :, :]), P[:, bank, :]).then_inc(z_ready[n], 1)

            def keep_hidden(group, k, bank):
                act.wait_ge(hid_psum[k], group.count)
                a.activation(hid[:, k, :], P[:, bank, :], ACT.Relu, bias=t["b1"][:, k:k + 1]).then_inc(hid_ready[k], 1)

            def slot(at, number):
                if at(1):
                    keep_hW(at(1))
                if at(0):
                    rstd_of(at(0), 0)
                if at(3):
                    keep_z(at(3), 1, B_EDGE)
                if at(1):
                    slope(at(1), 0)
                if at(2):
                    rstd_of(at(2), 1)
                if at(1):
                    slope(at(1), 1)
                if at(2):
                    normalise(at(2), 1)
                if at(1):
                    slope(at(1), 2)
                if at(0):
                    keep_hT(at(0))
                if at(2):
                    keep_z(at(2), 0, B_SUM)
                if at(1):
                    slope(at(1), 3)
                    exponential(at(1), 0)
                    exponential(at(1), 1)
                if at(2):
                    keep_hidden(at(2), 1, B_SUM)
                    keep_hidden(at(2), 0, B_TURN)
                if at(0):
                    keep_e(at(0))
                if at(3):
                    rstd_of(at(3), 3)
                if at(1):
                    keep_probT(at(1), 0)
                    exponential(at(1), 2)
                    exponential(at(1), 3)
                    keep_probT(at(1), 2)
                    keep_adjT(at(1))
                if at(2):
                    rstd_of(at(2), 2)
                    normalise(at(2), 2)
                if at(3):
                    keep_h0T(at(3))

            def keep_h0T(group):
                wait_apart(h0T_psum, group.count)
                a.activation(t["h0T"][:, group.all, :], P[:, B_TURN, :].rearrange("p (g n) -> p g n", g=GROUP),
                             ACT.Relu)\
                    .then_inc(h0T_kept, 1)

            act.preload_act_table_set("natural_log_exp_and_others")
            act.wait_ge(constants, 3)
            act.wait_ge(gru.loaded, gru.all_loaded)
            slots(act, slot)

        @block.vector
        def _(dve):
            v = nc.vector
            wait_apart = apart(dve, "vector")

            def moments(group, n, signal, count):
                wait_apart(signal, count)
                for g in range(GROUP):
                    last = v.bn_stats(stats[n][:, g, :], t["x"][:, group.graph(g), :])
                last.then_inc(stats_done[n], 1)
                wait_apart(stats_done[n], group.count)
                if n in (0, 3) and group.before(1).exists:
                    wait_apart(y_ready[n], group.before(1).count)
                for g in range(GROUP):
                    last = v.bn_aggr(mean_var[n][:, g, :], stats[n][:, g, :])
                last.then_inc(var_ready[n], 1)

            def shift_of(group, n):
                dve.wait_ge(rstd_ready[n], group.count)
                v.scalar_tensor_tensor(shift[n][:, :], mean_var[n][:, :, 0], -1.0, rstd[n][:, :], ALU.mult, ALU.mult)\
                    .then_inc(shift_ready[n], 1)

            def find_gone(group):
                dve.wait_ge(adj_loaded[group.odd], group.loads)
                if group.before(2).exists:
                    dve.wait_ge(score_ready, group.before(2).graph_count(GROUP - 1))
                v.tensor_scalar(gone[group.odd][:, :, :], adj[group.odd][:, :, :], 0.0, MASKED, ALU.is_le, ALU.mult)\
                    .then_inc(gone_ready, 1)

            def find_edges(group):
                wait_apart(adj_loaded[group.odd], group.loads)
                v.tensor_scalar(t["edges"][:, group.all, :], adj[group.odd][:, :, :], 0.0, None, ALU.not_equal)\
                    .then_inc(edges_ready, 1)

            def keep_e_lo(group):
                dve.wait_ge(e_hi, group.count)
                v.tensor_tensor(e_parts[group.odd][LO_ROW:2 * LO_ROW, :], P[LO_ROW:2 * LO_ROW, B_EDGE, :],
                                e_parts[group.odd][LO_ROW:2 * LO_ROW, :], ALU.subtract).then_inc(e_lo, 1)

            def leaky(group, g):
                row = prob[:, g, :, :].rearrange("p h m -> p (h m)")
                dve.wait_ge(sloped, group.graph_count(g))
                v.tensor_tensor(row, P[:, g, :], row, ALU.max).then_inc(lrelu_done, 1)

            def row_max(group, g):
                dve.wait_ge(lrelu_done, group.graph_count(g))
                v.tensor_reduce(top[:, g, :], prob[:, g, :, :], AXIS.X, ALU.max).then_inc(max_done, 1)

            def keep_probT(group, g):
                dve.wait_ge(probT_psum, group.graph_count(g))
                v.tensor_copy(probT[:, g, :, :].rearrange("p h n -> p (h n)"), P[:, g, :]).then_inc(probT_dve, 1)

            def divide(group):
                dve.wait_ge(att_psum, group.count)
                sums = P[:, 0:GROUP, 0:HEADS * (HEAD_DIM + 1)].rearrange("p g (h d) -> p g h d", h=HEADS)
                v.reciprocal(rsum[:, :, :], sums[:, :, :, HEAD_DIM]).then_inc(rsum_done, 1)
                dve.wait_ge(rsum_done, group.count)
                v.tensor_tensor(att[:, :, :, :], sums[:, :, :, 0:HEAD_DIM],
                                rsum[:, :, :].unsqueeze(3).to_broadcast([128, GROUP, HEADS, HEAD_DIM]),
                                ALU.mult).then_inc(att_done, 1)

            def add_attended(group):
                dve.wait_ge(att_done, group.count)
                v.tensor_tensor(xs(group), xs(group), att[:, :, :, :].rearrange("p g h d -> p g (h d)"), ALU.add)\
                    .then_inc(x_attended, 1)

            def add_out(group, n, bank):
                dve.wait_ge(out_psum[n], group.count)
                dve.wait_ge(biased[n], group.count)
                v.tensor_tensor(xs(group), P[:, bank, :].rearrange("p (g d) -> p g d", g=GROUP), xs(group), ALU.add)\
                    .then_inc(x_added[n], 1)

            def slot(at, number):
                if number == 0:
                    gru.keep(dve)
                elif number == 2:
                    gru.scale(dve)
                elif number == 3:
                    gru.split(dve)
                if at(3):
                    moments(at(3), 2, x_added[0], at(3).count)
                if at(2):
                    keep_probT(at(2), 3)
                if at(3):
                    shift_of(at(3), 2)
                if at(0):
                    moments(at(0), 0, x_loaded[at(0).odd], at(0).loads)
                if at(2):
                    divide(at(2))
                    add_attended(at(2))
                    moments(at(2), 1, x_attended, at(2).count)
                if at(1):
                    leaky(at(1), 0)
                if at(2):
                    shift_of(at(2), 1)
                if at(0):
                    find_gone(at(0))
                if at(1):
                    leaky(at(1), 1)
                if at(3):
                    add_out(at(3), 1, B_EDGE)
                if at(1):
                    row_max(at(1), 0)
                    row_max(at(1), 1)
                    leaky(at(1), 2)
                    row_max(at(1), 2)
                    leaky(at(1), 3)
                if at(3):
                    moments(at(3), 3, x_added[1], at(3).count)
                if at(1):
                    row_max(at(1), 3)
                    find_edges(at(1))
                if number == 0:
                    gru.keep_fused(dve)
                if at(0):
                    keep_e_lo(at(0))
                if number == 0:
                    gru.whole_max(dve)
                if at(1):
                    keep_probT(at(1), 1)
                if at(2):
                    add_out(at(2), 0, B_TURN)

            slots(dve, slot)


def gru_layer(nc, io, t, psum):
    with ExitStack() as ctx:
        def each(name, shape, dt=F32):
            return [ctx.enter_context(nc.sbuf_tensor(f"{name}{s}", shape, dt)) for s in range(STREAMS)]

        def sem(name):
            return ctx.enter_context(nc.semaphore(name))

        hp = each("h_parts", [128, 2, COLS], F16)
        hn = each("h_nodes", [128, 2, GROUP, DIM], F16)
        tp = each("t_parts", [128, 2, COLS], F16)
        r = each("r", [128, COLS])
        z = each("z", [128, COLS])
        zc = each("zc", [128, COLS])
        zh = each("zh", [128, COLS])
        cand = each("cand", [128, COLS])
        new = each("new", [128, COLS])
        final = each("final", [128, GROUP, NODES])
        out = each("out", [128, GROUP, DIM])

        hi_ready = sem("hi_ready")
        lo_ready = sem("lo_ready")
        turned = sem("turned")
        nodes_ready = sem("nodes_ready")
        t_psum = sem("t_psum")
        t_hi = sem("t_hi")
        t_lo = sem("t_lo")
        r_psum = sem("r_psum")
        z_psum = sem("z_psum_gru")
        h_share = sem("h_share")
        n_psum = sem("n_psum")
        r_ready = sem("r_ready")
        z_ready = sem("z_ready_gru")
        zc_ready = sem("zc_ready")
        zh_ready = sem("zh_ready")
        gated = sem("gated")
        summed = sem("summed")
        cand_ready = sem("cand_ready")
        mixed = sem("mixed")
        h_ready = sem("h_ready")
        passed = {e: sem(f"{e}_passed_gru") for e in ("vector", "gpsimd")}
        final_kept = sem("final_kept")
        back_psum = sem("back_psum")
        out_ready = sem("out_ready")
        stored = [sem(f"stored{s}") for s in range(STREAMS)]

        R, Z, N, T = range(BANKS)
        gb = t["gates_b"]

        def col(i):
            return gb[:, i:i + 1]

        class Slot:

            def __init__(self, p, i, s, back):
                self.now = (p, i, s)
                self.count = p * SLOTS + i * STREAMS + (s - back + 1)
                self.exists = not (isinstance(p, int) and isinstance(i, int)) or 0 < self.count <= SLOTS * ROUNDS
                if s < back:
                    s += STREAMS
                    if isinstance(i, int) and i == 0:
                        p, i = p - 1, GRU_STEPS
                    i = i - 1
                self.p, self.step, self.s = p, i, s - back
                self.bank = [psum[:, self.s % 2, b, :] for b in range(BANKS)]
                self.graph = p * (STREAMS * GROUP) + self.s * GROUP

        class Ended:

            def __init__(self, p, i, buffer):
                self.buffer = buffer
                self.count = p * STREAMS + i - STREAMS
                self.h_count = p * SLOTS + i
                self.first = p * (STREAMS * GROUP) + i * GROUP - (STREAMS + 1) * GROUP
                self.to_store = p * (16 * STREAMS) + i * 16 - 16 * STREAMS

        def group(p, s):
            return bass.ds(p * (STREAMS * GROUP) + s * GROUP, GROUP)

        def state(slot):
            return t["h0T"][:, group(slot.p, slot.s), :]

        def by_graph(x):
            return x.rearrange("p (g n) -> p g n", g=GROUP)

        def slots(eng, slot):
            def one_slot(p, i, s, copied=(), ended=None):
                def at(back):
                    found = Slot(p, i, s, back)
                    return found if found.exists else None
                slot(at, s, copied, ended)

            def first_step(p):
                for s in range(STREAMS):
                    one_slot(p, 0, s)

            first_step(0)
            with eng.Fori(1, GRU_STEPS) as i:
                for s in range(STREAMS):
                    one_slot(0, i, s)
            with eng.Fori(1, ROUNDS) as p:
                first_step(p)
                with eng.Fori(1, GRU_STEPS) as i:
                    group = Ended(p, i, 0)
                    one_slot(p, i, 0, copied=[group])
                    one_slot(p, i, 1, ended=group)
                    one_slot(p, i, 2)
                    one_slot(p, i, 3)
            last = [Ended(ROUNDS, s + 1, s) for s in range(STREAMS)]
            for s in range(STREAMS):
                one_slot(ROUNDS, 0, s, copied=last[:2] if s == 0 else last[s + 1:s + 2], ended=last[s])

        block = ctx.enter_context(nc.Block())

        @block.tensor
        def _(pe):
            def gate(bank, which, step, parts, start=False, stop=False):
                for n, (w, m) in enumerate([(0, 0), (1, 0), (0, 1)]):
                    last = mm(nc, bank, t["gru_w"][:, w, step, which * DIM:(which + 1) * DIM], parts[:, m, :],
                              start and n == 0, stop and n == 2)
                return last

            def turn_parts(now, two_before):
                turn = now.bank[T].bitcast(F16).rearrange("p (m g c) -> p m g c", m=2, g=GROUP)
                if two_before:
                    pe.wait_ge(summed, two_before.count)
                pe.wait_ge(hi_ready, now.count)
                for m in range(2):
                    if m == 1:
                        pe.wait_ge(lo_ready, now.count)
                    for g in range(GROUP):
                        last = nc.tensor.transpose(turn[:, m, g, :], hp[now.s][:, m, g * 128:(g + 1) * 128],
                                                   t["ident16"][:, :])
                last.then_inc(turned, 1)

            def neighbours(now):
                pe.wait_ge(nodes_ready, now.count)
                for g in range(GROUP):
                    for m in range(2):
                        last = mm(nc, now.bank[T][:, g * 128:(g + 1) * 128], hn[now.s][:, m, g, :],
                                  t["edges"][:, now.graph + g, :], m == 0, m == 1)
                last.then_inc(t_psum, 1)

            def back(group, s, two_before):
                pe.wait_ge(final_kept, group.count)
                if two_before:
                    pe.wait_ge(gated, two_before.count)
                else:
                    pe.wait_ge(out_ready, group.count - 2)
                for g in range(GROUP):
                    last = nc.tensor.transpose(psum[:, s % 2, N, g * 128:(g + 1) * 128],
                                               final[group.buffer][:, g, :], t["ident"][:, :])
                last.then_inc(back_psum, 1)

            def slot(at, s, copied, ended):
                two_before = at(2)
                if at(0):
                    turn_parts(at(0), two_before)
                if at(1):
                    pe.wait_ge(t_lo, at(1).count)
                    gate(at(1).bank[R], 0, at(1).step, tp[at(1).s], stop=True).then_inc(r_psum, 1)
                    gate(at(1).bank[T], 2, at(1).step, tp[at(1).s], start=True, stop=True).then_inc(n_psum, 1)
                if ended is not None:
                    back(ended, s, two_before)
                if at(0):
                    if two_before:
                        pe.wait_ge(zc_ready, two_before.count)
                    gate(at(0).bank[Z], 1, GRU_STEPS, hp[s], start=True)
                    neighbours(at(0))
                if at(1):
                    gate(at(1).bank[Z], 1, at(1).step, tp[at(1).s], stop=True).then_inc(z_psum, 1)
                if at(0):
                    if two_before:
                        pe.wait_ge(r_ready, two_before.count)
                    gate(at(0).bank[R], 0, GRU_STEPS, hp[s], start=True)
                    if ended is not None:
                        pe.wait_ge(out_ready, ended.count)
                    gate(at(0).bank[N], 2, GRU_STEPS, hp[s], start=True, stop=True).then_inc(h_share, 1)

            slots(pe, slot)

        @block.scalar
        def _(act):
            a = nc.scalar

            def keep_final(group):
                act.wait_ge(h_ready, group.h_count)
                a.copy(final[group.buffer][:, :, :], t["h0T"][:, bass.ds(group.first, GROUP), :])\
                    .then_inc(final_kept, 1)

            def slot(at, s, copied, ended):
                if ended in copied:
                    keep_final(ended)
                if at(0):
                    act.wait_ge(t_psum, at(0).count)
                    a.copy(tp[s][:, 0, :], at(0).bank[T]).then_inc(t_hi, 1)
                if at(1):
                    one = at(1)
                    act.wait_ge(z_psum, one.count)
                    a.activation(z[one.s][:, :], one.bank[Z], ACT.Sigmoid, bias=col(B_Z), scale=col(UNSCALE))\
                        .then_inc(z_ready, 1)
                    a.activation(zc[one.s][:, :], one.bank[Z], ACT.Sigmoid, bias=col(B_NZ), scale=col(N_UNSCALE))\
                        .then_inc(zc_ready, 1)
                    act.wait_ge(summed, one.count)
                    a.activation(cand[one.s][:, :], new[one.s][:, :], ACT.Tanh, bias=col(B_IN), scale=col(UNSCALE))\
                        .then_inc(cand_ready, 1)
                for group in copied:
                    if group is not ended:
                        keep_final(group)
                if at(0):
                    act.wait_ge(r_psum, at(0).count)
                    a.activation(r[s][:, :], at(0).bank[R], ACT.Sigmoid, bias=col(B_R), scale=col(UNSCALE))\
                        .then_inc(r_ready, 1)

            act.preload_act_table_set("sigmoid_and_others")
            slots(act, slot)

        @block.gpsimd
        def _(pool):
            def slot(at, s, copied, ended):
                if at(0):
                    now = at(0)
                    pool.wait_ge(z_ready, now.count)
                    pool.sem_inc(passed["gpsimd"], 1)
                    pool.tensor_tensor(by_graph(zh[s][:, :]), by_graph(z[s][:, :]), state(now), ALU.mult)\
                        .then_inc(zh_ready, 1)
                    pool.wait_ge(mixed, now.count)
                    pool.wait_ge(zh_ready, now.count)
                    pool.sem_inc(passed["gpsimd"], 1)
                    pool.tensor_tensor(state(now), by_graph(cand[s][:, :]), by_graph(zh[s][:, :]), ALU.add)\
                        .then_inc(h_ready, 1)

            pool.sem_inc(h_ready, STREAMS)
            slots(pool, slot)

        @block.vector
        def _(dve):
            v = nc.vector

            def finish(group, s):
                dve.wait_ge(back_psum, group.count)
                if group.buffer == 0:
                    dve.wait_ge(stored[0], group.to_store)
                for g in range(GROUP):
                    last = v.scalar_tensor_tensor(out[group.buffer][:, g, :], psum[:, s % 2, N, g * 128:(g + 1) * 128],
                                                  t["mask"][:, bass.ds(group.first + g, 1)],
                                                  t["x"][:, group.first + g, :], ALU.mult, ALU.add)
                last.then_inc(out_ready, 1)

            def slot(at, s, copied, ended):
                if at(0):
                    dve.wait_ge(h_ready, at(0).count)
                    dve.sem_inc(passed["vector"], 1)
                    v.tensor_copy(by_graph(hp[s][:, 0, :]), state(at(0))).then_inc(hi_ready, 1)
                if at(2):
                    two = at(2)
                    dve.wait_ge(gated, two.count)
                    dve.wait_ge(n_psum, two.count)
                    v.tensor_tensor(new[two.s][:, :], two.bank[T], r[two.s][:, :], ALU.add).then_inc(summed, 1)
                if at(0):
                    dve.wait_ge(hi_ready, at(0).count)
                    v.tensor_tensor(by_graph(hp[s][:, 1, :]), state(at(0)), by_graph(hp[s][:, 0, :]), ALU.subtract)\
                        .then_inc(lo_ready, 1)
                if at(1):
                    one = at(1)
                    dve.wait_ge(t_hi, one.count)
                    v.tensor_tensor(tp[one.s][:, 1, :], one.bank[T], tp[one.s][:, 0, :], ALU.subtract).then_inc(t_lo, 1)
                if at(0):
                    dve.wait_ge(turned, at(0).count)
                    v.tensor_copy(hn[s][:, :, :, :].rearrange("p m g c -> p (m g c)"), at(0).bank[T].bitcast(F16))\
                        .then_inc(nodes_ready, 1)
                if at(2):
                    two = at(2)
                    dve.wait_ge(cand_ready, two.count)
                    dve.wait_ge(zc_ready, two.count)
                    v.tensor_tensor(cand[two.s][:, :], cand[two.s][:, :], zc[two.s][:, :], ALU.mult).then_inc(mixed, 1)
                if at(1):
                    one = at(1)
                    dve.wait_ge(r_ready, one.count)
                    dve.wait_ge(h_share, one.count)
                    v.scalar_tensor_tensor(r[one.s][:, :], one.bank[N], col(B_HN), r[one.s][:, :], ALU.add, ALU.mult)\
                        .then_inc(gated, 1)
                if ended is not None:
                    finish(ended, s)

            dve.sem_inc(stored[0], 16)
            slots(dve, slot)

        @block.sync
        def _(sp):
            def store(number, s):
                sp.wait_ge(out_ready, number + 1)
                sp.dma_start(io["out"][bass.ds(number * GROUP, GROUP)].rearrange("g n d -> n g d"), out[s][:, :, :])\
                    .then_inc(stored[s], 16)

            early = GROUPS - STREAMS
            with sp.Fori(0, early) as number:
                store(number, 0)
            for s in range(STREAMS):
                store(early + s, s)
            sp.wait_ge(stored[0], 16 + 16 * (early + 1))
            for s in range(1, STREAMS):
                sp.wait_ge(stored[s], 16)


NAMES = ["x", "adj", "nodemask", "L0_gnn_W", "L0_gnn_a", "L1_gnn_eps", "L1_gnn_W1", "L1_gnn_b1", "L1_gnn_W2",
         "L1_gnn_b2", "L2_gnn_weight", "L2_gnn_bias", "L3_gnn_weight", "L3_gnn_w_ih", "L3_gnn_w_hh", "L3_gnn_b_ih",
         "L3_gnn_b_hh"]


def kernel(**inputs):
    import numpy as np
    import concourse.bacc as bacc
    from concourse.bass_utils import run_bass_kernel_spmd

    nc = bacc.Bacc("TRN2", target_bir_lowering=False, num_devices=1)
    arrays, io = {}, {}
    for name in NAMES:
        a = np.ascontiguousarray(inputs[name])
        arrays[f"in_{name}"] = a
        io[name] = nc.dram_tensor(f"in_{name}", a.shape, mybir.dt.from_np(a.dtype), kind="ExternalInput").ap()
    io["out"] = nc.dram_tensor("out_x", (GRAPHS, NODES, DIM), F32, kind="ExternalOutput").ap()
    build(nc, io)
    got = run_bass_kernel_spmd(nc, [arrays], core_ids=[0])
    return got.results[0]["out_x"]
```
